# Optimizing a Trainium2 kernel written in Bass

```python
import numpy as np
import jax
import jax.numpy as jnp

def _softmax(x, axis=-1):
    return jax.nn.softmax(x, axis=axis)

def _gelu(x):
    return jax.nn.gelu(x, approximate=True)

def _silu(x):
    return jax.nn.silu(x)

def _sigmoid(x):
    return jax.nn.sigmoid(x)

def _layernorm(x, axis=-1, eps=1e-05):
    m = jnp.mean(x, axis=axis, keepdims=True)
    v = jnp.var(x, axis=axis, keepdims=True)
    return (x - m) / jnp.sqrt(v + eps)

def _scatter_add(tgt, idx, src, axis=0):
    return tgt.at[idx].add(src)

def _segment_sum(src, seg, n):
    return jax.ops.segment_sum(src, seg, n)
kernel_name = 'mk_gnn_preln_d4_gnn_r32_17946b'

def setup_inputs(seed: int=0):
    np.random.seed(seed)
    _w = jnp.asarray

    def _rec_inputs():
        import jax
        import jax.numpy as jnp
        _gk = jax.random.key(seed)
        x = -0.000202 + 1 * jax.random.normal(jax.random.fold_in(_gk, 1), (3125, 128), jnp.float32)
        _s = jax.random.randint(jax.random.fold_in(_gk, 2), (25000,), 0, 3125, jnp.int32)
        _d = jax.random.randint(jax.random.fold_in(_gk, 3), (25000,), 0, 3125, jnp.int32)
        _loop = jnp.arange(3125, dtype=jnp.int32)
        src = jnp.concatenate([_s, _d, _loop])
        dst = jnp.concatenate([_d, _s, _loop])
        _o = jnp.argsort(dst, stable=True)
        src = src[_o]
        dst = dst[_o]
        edge_attr_64 = 0.000189758 + 1.00013 * jax.random.normal(jax.random.fold_in(_gk, 13), (53125, 64), jnp.float32)
        edge_weight1 = jax.random.uniform(jax.random.fold_in(_gk, 15), (53125, 1), jnp.float32, 0.0, 0.999998)
        return (x, src, dst, edge_attr_64, edge_weight1)
    x, src, dst, edge_attr_64, edge_weight1 = _rec_inputs()

    def _L0_gnn_setup():
        import jax, jax.numpy as jnp
        import numpy as np
        N_NODES = 50000
        N_EDGES = 25000
        IN_DIM = 128
        HIDDEN = 32
        HEADS = 4
        NEG_SLOPE = 0.2

        def _gat_conv(x, W, a_src, a_dst, bias, src, dst, n_nodes):
            H, C = a_src.shape
            h = (x @ W).reshape(n_nodes, H, C)
            alpha_s = jnp.sum(h * a_src, axis=-1)
            alpha_d = jnp.sum(h * a_dst, axis=-1)
            e = jax.nn.leaky_relu(alpha_s[src] + alpha_d[dst], NEG_SLOPE)
            m = jax.ops.segment_max(e, dst, num_segments=n_nodes)
            e = jnp.exp(e - m[dst])
            z = jax.ops.segment_sum(e, dst, num_segments=n_nodes)
            alpha = e / (z[dst] + 1e-16)
            msg = alpha[:, :, None] * h[src]
            out = jax.ops.segment_sum(msg, dst, num_segments=n_nodes)
            return out.reshape(n_nodes, H * C) + bias
        key = jax.random.key(seed)
        ks = jax.random.split(key, 12)
        x = jax.random.normal(ks[0], (N_NODES, IN_DIM), dtype=jnp.float32)
        edge_index = jax.random.randint(ks[1], (2, N_EDGES), 0, N_NODES, dtype=jnp.int64) if jax.config.read('jax_enable_x64') else jax.random.randint(ks[1], (2, N_EDGES), 0, N_NODES).astype(jnp.int32)
        d1 = HEADS * HIDDEN
        sc1 = 1.0 / np.sqrt(IN_DIM)
        sc2 = 1.0 / np.sqrt(d1)
        W1 = jax.random.normal(ks[2], (IN_DIM, d1), dtype=jnp.float32) * sc1
        a_src1 = jax.random.normal(ks[3], (HEADS, HIDDEN), dtype=jnp.float32) * 0.1
        a_dst1 = jax.random.normal(ks[4], (HEADS, HIDDEN), dtype=jnp.float32) * 0.1
        b1 = jnp.zeros((d1,), dtype=jnp.float32)
        W2 = jax.random.normal(ks[5], (d1, d1), dtype=jnp.float32) * sc2
        a_src2 = jax.random.normal(ks[6], (HEADS, HIDDEN), dtype=jnp.float32) * 0.1
        a_dst2 = jax.random.normal(ks[7], (HEADS, HIDDEN), dtype=jnp.float32) * 0.1
        b2 = jnp.zeros((d1,), dtype=jnp.float32)
        return {'x': x, 'edge_index': edge_index, 'W1': W1, 'a_src1': a_src1, 'a_dst1': a_dst1, 'b1': b1, 'W2': W2, 'a_src2': a_src2, 'a_dst2': a_dst2, 'b2': b2}
    _L0_gnn_all = _L0_gnn_setup()
    _L0_gnn_in = {k: v for k, v in _L0_gnn_all.items() if k in ('W1', 'a_src1', 'a_dst1', 'b1', 'W2', 'a_src2', 'a_dst2', 'b2')}
    del _L0_gnn_all

    def _L1_gnn_setup():
        import jax, jax.numpy as jnp
        import numpy as np
        N_NODES = 50000
        N_EDGES = 18750
        IN_FEATS = 128
        OUT_FEATS = 128
        key = jax.random.key(seed)
        k_h, k_norm, k_src, k_dst, k_ew, k_w, k_b = jax.random.split(key, 7)
        h = jax.random.normal(k_h, (N_NODES, IN_FEATS), dtype=jnp.float32)
        norm = jax.random.uniform(k_norm, (N_NODES, 1), dtype=jnp.float32)
        edge_src = jax.random.randint(k_src, (N_EDGES,), 0, N_NODES, dtype=jnp.int32)
        edge_dst = jax.random.randint(k_dst, (N_EDGES,), 0, N_NODES, dtype=jnp.int32)
        edge_weight = jax.random.uniform(k_ew, (N_EDGES, 1), dtype=jnp.float32)
        stdv = 1.0 / np.sqrt(OUT_FEATS)
        W = jax.random.uniform(k_w, (IN_FEATS, OUT_FEATS), dtype=jnp.float32, minval=-stdv, maxval=stdv)
        b = jax.random.uniform(k_b, (OUT_FEATS,), dtype=jnp.float32, minval=-stdv, maxval=stdv)
        return {'h': h, 'norm': norm, 'edge_src': edge_src, 'edge_dst': edge_dst, 'edge_weight': edge_weight, 'W': W, 'b': b}
    _L1_gnn_all = _L1_gnn_setup()
    _L1_gnn_in = {k: v for k, v in _L1_gnn_all.items() if k in ('W', 'b')}
    del _L1_gnn_all

    def _L2_gnn_setup():
        import jax, jax.numpy as jnp
        import numpy as np
        N, E, IN_DIM, OUT_DIM, EDGE_DIM, HEADS = (50000, 25000, 128, 128, 64, 4)
        C = OUT_DIM // HEADS
        NEG_SLOPE = 0.2
        EPS = 1e-05

        def _gatv2_graphnorm(x, edge_index, edge_attr, Wl, bl, Wr, br, We, att, bias_out, gn_weight, gn_bias, gn_mean_scale):
            src, dst = (edge_index[0], edge_index[1])
            n = x.shape[0]
            deg = jax.ops.segment_sum(jnp.ones((edge_attr.shape[0],), x.dtype), dst, num_segments=n)
            loop_attr = jax.ops.segment_sum(edge_attr, dst, num_segments=n) / jnp.maximum(deg, 1.0)[:, None]
            loop = jnp.arange(n, dtype=src.dtype)
            src_a = jnp.concatenate([src, loop])
            dst_a = jnp.concatenate([dst, loop])
            eattr = jnp.concatenate([edge_attr, loop_attr], axis=0)
            xl = (x @ Wl + bl).reshape(n, HEADS, C)
            xr = (x @ Wr + br).reshape(n, HEADS, C)
            ee = (eattr @ We).reshape(-1, HEADS, C)
            msg = xl[src_a] + xr[dst_a] + ee
            score = jnp.einsum('ehc,hc->eh', jax.nn.leaky_relu(msg, NEG_SLOPE), att)
            smax = jax.ops.segment_max(score, dst_a, num_segments=n)
            ex = jnp.exp(score - smax[dst_a])
            denom = jax.ops.segment_sum(ex, dst_a, num_segments=n)
            alpha = ex / (denom[dst_a] + 1e-16)
            out = jax.ops.segment_sum(alpha[:, :, None] * xl[src_a], dst_a, num_segments=n)
            out = out.reshape(n, HEADS * C) + bias_out
            mean = out.mean(axis=0)
            o = out - mean * gn_mean_scale
            var = (o * o).mean(axis=0)
            out = gn_weight * o / jnp.sqrt(var + EPS) + gn_bias
            return jax.nn.relu(out)
        key = jax.random.key(seed)
        ks = jax.random.split(key, 12)
        x = jax.random.normal(ks[0], (N, IN_DIM), dtype=jnp.float32)
        edge_index = jax.random.randint(ks[1], (2, E), 0, N, dtype=jnp.int64)
        edge_attr = jax.random.normal(ks[2], (E, EDGE_DIM), dtype=jnp.float32)
        s = 0.05
        Wl = jax.random.normal(ks[3], (IN_DIM, HEADS * C), dtype=jnp.float32) * s
        bl = jnp.zeros((HEADS * C,), dtype=jnp.float32)
        Wr = jax.random.normal(ks[4], (IN_DIM, HEADS * C), dtype=jnp.float32) * s
        br = jnp.zeros((HEADS * C,), dtype=jnp.float32)
        We = jax.random.normal(ks[5], (EDGE_DIM, HEADS * C), dtype=jnp.float32) * s
        att = jax.random.normal(ks[6], (HEADS, C), dtype=jnp.float32) * s
        bias_out = jnp.zeros((HEADS * C,), dtype=jnp.float32)
        gn_weight = jnp.ones((OUT_DIM,), dtype=jnp.float32)
        gn_bias = jnp.zeros((OUT_DIM,), dtype=jnp.float32)
        gn_mean_scale = jnp.ones((OUT_DIM,), dtype=jnp.float32)
        return dict(x=x, edge_index=edge_index, edge_attr=edge_attr, Wl=Wl, bl=bl, Wr=Wr, br=br, We=We, att=att, bias_out=bias_out, gn_weight=gn_weight, gn_bias=gn_bias, gn_mean_scale=gn_mean_scale)
    _L2_gnn_all = _L2_gnn_setup()
    _L2_gnn_in = {k: v for k, v in _L2_gnn_all.items() if k in ('Wl', 'bl', 'Wr', 'br', 'We', 'att', 'bias_out', 'gn_weight', 'gn_bias', 'gn_mean_scale')}
    del _L2_gnn_all

    def _L3_gnn_setup():
        import jax, jax.numpy as jnp
        import numpy as np
        N = 50000
        E = 25000
        HIDDEN = 128
        NUM_HEADS = 8
        D_HEAD = HIDDEN // NUM_HEADS
        key = jax.random.key(seed)
        ks = jax.random.split(key, 12)
        sc = 1.0 / np.sqrt(HIDDEN)
        inp = {'h': jax.random.normal(ks[0], (N, HIDDEN), dtype=jnp.float32), 'rows': jax.random.randint(ks[1], (E,), 0, N, dtype=jnp.int32), 'cols': jax.random.randint(ks[2], (E,), 0, N, dtype=jnp.int32), 'Wq': jax.random.normal(ks[3], (HIDDEN, HIDDEN), dtype=jnp.float32) * sc, 'bq': jax.random.normal(ks[4], (HIDDEN,), dtype=jnp.float32) * sc, 'Wk': jax.random.normal(ks[5], (HIDDEN, HIDDEN), dtype=jnp.float32) * sc, 'bk': jax.random.normal(ks[6], (HIDDEN,), dtype=jnp.float32) * sc, 'Wv': jax.random.normal(ks[7], (HIDDEN, HIDDEN), dtype=jnp.float32) * sc, 'bv': jax.random.normal(ks[8], (HIDDEN,), dtype=jnp.float32) * sc, 'Wo': jax.random.normal(ks[9], (HIDDEN, HIDDEN), dtype=jnp.float32) * sc, 'bo': jax.random.normal(ks[10], (HIDDEN,), dtype=jnp.float32) * sc}
        return inp
    _L3_gnn_all = _L3_gnn_setup()
    _L3_gnn_in = {k: v for k, v in _L3_gnn_all.items() if k in ('Wq', 'bq', 'Wk', 'bk', 'Wv', 'bv', 'Wo', 'bo')}
    del _L3_gnn_all
    return {'x': x, 'src': src, 'dst': dst, 'edge_attr_64': edge_attr_64, 'edge_weight1': edge_weight1, 'L0_gnn_W1': _L0_gnn_in['W1'], 'L0_gnn_a_src1': _L0_gnn_in['a_src1'], 'L0_gnn_a_dst1': _L0_gnn_in['a_dst1'], 'L0_gnn_b1': _L0_gnn_in['b1'], 'L0_gnn_W2': _L0_gnn_in['W2'], 'L0_gnn_a_src2': _L0_gnn_in['a_src2'], 'L0_gnn_a_dst2': _L0_gnn_in['a_dst2'], 'L0_gnn_b2': _L0_gnn_in['b2'], 'L1_gnn_W': _L1_gnn_in['W'], 'L1_gnn_b': _L1_gnn_in['b'], 'L2_gnn_Wl': _L2_gnn_in['Wl'], 'L2_gnn_bl': _L2_gnn_in['bl'], 'L2_gnn_Wr': _L2_gnn_in['Wr'], 'L2_gnn_br': _L2_gnn_in['br'], 'L2_gnn_We': _L2_gnn_in['We'], 'L2_gnn_att': _L2_gnn_in['att'], 'L2_gnn_bias_out': _L2_gnn_in['bias_out'], 'L2_gnn_gn_weight': _L2_gnn_in['gn_weight'], 'L2_gnn_gn_bias': _L2_gnn_in['gn_bias'], 'L2_gnn_gn_mean_scale': _L2_gnn_in['gn_mean_scale'], 'L3_gnn_Wq': _L3_gnn_in['Wq'], 'L3_gnn_bq': _L3_gnn_in['bq'], 'L3_gnn_Wk': _L3_gnn_in['Wk'], 'L3_gnn_bk': _L3_gnn_in['bk'], 'L3_gnn_Wv': _L3_gnn_in['Wv'], 'L3_gnn_bv': _L3_gnn_in['bv'], 'L3_gnn_Wo': _L3_gnn_in['Wo'], 'L3_gnn_bo': _L3_gnn_in['bo']}

def reference(x, src, dst, edge_attr_64, edge_weight1, L0_gnn_W1, L0_gnn_a_src1, L0_gnn_a_dst1, L0_gnn_b1, L0_gnn_W2, L0_gnn_a_src2, L0_gnn_a_dst2, L0_gnn_b2, L1_gnn_W, L1_gnn_b, L2_gnn_Wl, L2_gnn_bl, L2_gnn_Wr, L2_gnn_br, L2_gnn_We, L2_gnn_att, L2_gnn_bias_out, L2_gnn_gn_weight, L2_gnn_gn_bias, L2_gnn_gn_mean_scale, L3_gnn_Wq, L3_gnn_bq, L3_gnn_Wk, L3_gnn_bk, L3_gnn_Wv, L3_gnn_bv, L3_gnn_Wo, L3_gnn_bo):
    import jax
    import jax.numpy as jnp

    def _L0_gnn_ref(x, edge_index, W1, a_src1, a_dst1, b1, W2, a_src2, a_dst2, b2):
        import jax, jax.numpy as jnp
        import numpy as np
        N_NODES = 50000
        N_EDGES = 25000
        IN_DIM = 128
        HIDDEN = 32
        HEADS = 4
        NEG_SLOPE = 0.2

        def _gat_conv(x, W, a_src, a_dst, bias, src, dst, n_nodes):
            H, C = a_src.shape
            h = (x @ W).reshape(n_nodes, H, C)
            alpha_s = jnp.sum(h * a_src, axis=-1)
            alpha_d = jnp.sum(h * a_dst, axis=-1)
            e = jax.nn.leaky_relu(alpha_s[src] + alpha_d[dst], NEG_SLOPE)
            m = jax.ops.segment_max(e, dst, num_segments=n_nodes)
            e = jnp.exp(e - m[dst])
            z = jax.ops.segment_sum(e, dst, num_segments=n_nodes)
            alpha = e / (z[dst] + 1e-16)
            msg = alpha[:, :, None] * h[src]
            out = jax.ops.segment_sum(msg, dst, num_segments=n_nodes)
            return out.reshape(n_nodes, H * C) + bias
        n = x.shape[0]
        loops = jnp.arange(n, dtype=edge_index.dtype)
        src = jnp.concatenate([edge_index[0], loops])
        dst = jnp.concatenate([edge_index[1], loops])
        h = _gat_conv(x, W1, a_src1, a_dst1, b1, src, dst, n)
        h = jax.nn.relu(h)
        out = _gat_conv(h, W2, a_src2, a_dst2, b2, src, dst, n)
        return out

    def _L1_gnn_ref(h, norm, edge_src, edge_dst, edge_weight, W, b):
        import jax, jax.numpy as jnp
        import numpy as np
        N_NODES = 50000
        N_EDGES = 18750
        IN_FEATS = 128
        OUT_FEATS = 128
        hw = jnp.matmul(h, W)
        msg = norm[edge_src] * hw[edge_src] * edge_weight
        agg = jax.ops.segment_sum(msg, edge_dst, num_segments=h.shape[0])
        out = agg * norm + b
        return jax.nn.relu(out)

    def _L2_gnn_ref(x, edge_index, edge_attr, Wl, bl, Wr, br, We, att, bias_out, gn_weight, gn_bias, gn_mean_scale):
        import jax, jax.numpy as jnp
        import numpy as np
        N, E, IN_DIM, OUT_DIM, EDGE_DIM, HEADS = (50000, 25000, 128, 128, 64, 4)
        C = OUT_DIM // HEADS
        NEG_SLOPE = 0.2
        EPS = 1e-05

        def _gatv2_graphnorm(x, edge_index, edge_attr, Wl, bl, Wr, br, We, att, bias_out, gn_weight, gn_bias, gn_mean_scale):
            src, dst = (edge_index[0], edge_index[1])
            n = x.shape[0]
            deg = jax.ops.segment_sum(jnp.ones((edge_attr.shape[0],), x.dtype), dst, num_segments=n)
            loop_attr = jax.ops.segment_sum(edge_attr, dst, num_segments=n) / jnp.maximum(deg, 1.0)[:, None]
            loop = jnp.arange(n, dtype=src.dtype)
            src_a = jnp.concatenate([src, loop])
            dst_a = jnp.concatenate([dst, loop])
            eattr = jnp.concatenate([edge_attr, loop_attr], axis=0)
            xl = (x @ Wl + bl).reshape(n, HEADS, C)
            xr = (x @ Wr + br).reshape(n, HEADS, C)
            ee = (eattr @ We).reshape(-1, HEADS, C)
            msg = xl[src_a] + xr[dst_a] + ee
            score = jnp.einsum('ehc,hc->eh', jax.nn.leaky_relu(msg, NEG_SLOPE), att)
            smax = jax.ops.segment_max(score, dst_a, num_segments=n)
            ex = jnp.exp(score - smax[dst_a])
            denom = jax.ops.segment_sum(ex, dst_a, num_segments=n)
            alpha = ex / (denom[dst_a] + 1e-16)
            out = jax.ops.segment_sum(alpha[:, :, None] * xl[src_a], dst_a, num_segments=n)
            out = out.reshape(n, HEADS * C) + bias_out
            mean = out.mean(axis=0)
            o = out - mean * gn_mean_scale
            var = (o * o).mean(axis=0)
            out = gn_weight * o / jnp.sqrt(var + EPS) + gn_bias
            return jax.nn.relu(out)
        return _gatv2_graphnorm(x, edge_index, edge_attr, Wl, bl, Wr, br, We, att, bias_out, gn_weight, gn_bias, gn_mean_scale)

    def _L3_gnn_ref(h, rows, cols, Wq, bq, Wk, bk, Wv, bv, Wo, bo):
        import jax, jax.numpy as jnp
        import numpy as np
        N = 50000
        E = 25000
        HIDDEN = 128
        NUM_HEADS = 8
        D_HEAD = HIDDEN // NUM_HEADS
        n = h.shape[0]
        scaling = D_HEAD ** (-0.5)
        q = (h @ Wq.T + bq).reshape(n, D_HEAD, NUM_HEADS) * scaling
        k = (h @ Wk.T + bk).reshape(n, D_HEAD, NUM_HEADS)
        v = (h @ Wv.T + bv).reshape(n, D_HEAD, NUM_HEADS)
        scores = jnp.einsum('edh,edh->eh', q[rows], k[cols])
        m = jax.ops.segment_max(scores, rows, num_segments=n)
        e = jnp.exp(scores - m[rows])
        s = jax.ops.segment_sum(e, rows, num_segments=n)
        attn = e / s[rows]
        out = jax.ops.segment_sum(attn[:, None, :] * v[cols], rows, num_segments=n)
        return out.reshape(n, HIDDEN) @ Wo.T + bo
    edge_index = jnp.stack([src, dst])
    deg = jnp.maximum(jax.ops.segment_sum(jnp.ones(dst.shape, jnp.float32), dst, num_segments=3125), 1.0)
    deg_isqrt = deg ** (-0.5)
    h = jnp.maximum(_layernorm(x, axis=-1), 0.0)
    x = x + _L0_gnn_ref(h, edge_index, L0_gnn_W1, L0_gnn_a_src1, L0_gnn_a_dst1, L0_gnn_b1, L0_gnn_W2, L0_gnn_a_src2, L0_gnn_a_dst2, L0_gnn_b2)
    h = jnp.maximum(_layernorm(x, axis=-1), 0.0)
    x = x + _L1_gnn_ref(h, deg_isqrt[:, None], src, dst, edge_weight1, L1_gnn_W, L1_gnn_b)
    h = jnp.maximum(_layernorm(x, axis=-1), 0.0)
    x = x + _L2_gnn_ref(h, edge_index, edge_attr_64, L2_gnn_Wl, L2_gnn_bl, L2_gnn_Wr, L2_gnn_br, L2_gnn_We, L2_gnn_att, L2_gnn_bias_out, L2_gnn_gn_weight, L2_gnn_gn_bias, L2_gnn_gn_mean_scale)
    h = jnp.maximum(_layernorm(x, axis=-1), 0.0)
    x = x + _L3_gnn_ref(h, src, dst, L3_gnn_Wq, L3_gnn_bq, L3_gnn_Wk, L3_gnn_bk, L3_gnn_Wv, L3_gnn_bv, L3_gnn_Wo, L3_gnn_bo)
    return x

_drawn_inputs = setup_inputs


def setup_inputs(seed=0):
    import zlib

    import numpy as np

    out = dict(_drawn_inputs(seed))
    spreads = {'L0_gnn_b1': (0.0, 0.1),
     'L0_gnn_b2': (0.0, 0.1),
     'L2_gnn_bl': (0.0, 0.1),
     'L2_gnn_br': (0.0, 2.0),
     'L2_gnn_bias_out': (0.0, 0.1),
     'L2_gnn_gn_weight': (1.0, 0.2),
     'L2_gnn_gn_bias': (0.0, 0.1),
     'L2_gnn_gn_mean_scale': (1.0, 0.2)}
    factors = {'edge_weight1': 3.122,
     'L0_gnn_a_dst1': 64.0,
     'L0_gnn_a_src2': 38.302,
     'L0_gnn_a_dst2': 176.34,
     'L2_gnn_Wr': 11.146,
     'L3_gnn_bq': 8.0,
     'L3_gnn_bk': 200.0,
     'L0_gnn_a_src1': 3.149}
    for name, (base, spread) in spreads.items():
        noise = np.random.default_rng([zlib.crc32(name.encode()), seed]).standard_normal(out[name].shape)
        drawn = base * np.exp(spread * noise) if base else spread * noise
        out[name] = jnp.asarray(drawn.astype(out[name].dtype))
    for name, factor in factors.items():
        out[name] = (out[name] * factor).astype(out[name].dtype)
    return out
```

```python
from contextlib import ExitStack

import concourse.bass as bass
from concourse import mybir

ALU = mybir.AluOpType
ACT = mybir.ActivationFunctionType
AX_X = mybir.AxisListType.X
F32 = mybir.dt.float32
I32 = mybir.dt.int32
BF16 = mybir.dt.bfloat16

P = 128
NODES = 3125
EDGES = 53125
D = 128
ED = 64
NP = 125
NI = NODES // NP
GT = 16
TILES = -(-EDGES // (P * GT)) * GT
GROUPS = TILES // GT
EPAD = TILES * P
TROWS = NODES + P
CH = 448
NCH = 7
NCOL = NCH * CH
ACOL = GROUPS * P
BIG = 1e38
NEG = 0.2
EPS = 1e-5
TB = 4
NB = -(-NI // TB)
TC = 5
VROW = 256
assert NP * NI == NODES and TILES == ACOL // P * GT and GROUPS % 2 == 0 and NCOL + P <= ACOL

GAT1, GAT2, GCN, GATV2, ATTN = range(5)
SOFTMAX = (GAT1, GAT2, GATV2, ATTN)
LN_OF = {GAT1: 0, GCN: 1, GATV2: 2, ATTN: 3}
HEADS = {GAT1: 4, GAT2: 4, GATV2: 4, ATTN: 8}
TF = {GAT1: 136, GAT2: 136, GCN: 128, GATV2: 256, ATTN: 384}
ROWF = {GAT1: 132, GAT2: 132, GCN: 128, GATV2: 128, ATTN: 256}
WINF = {GAT1: 4, GAT2: 4, GATV2: 128, ATTN: 128}
VOFF = {GAT1: 0, GAT2: 0, GCN: 0, GATV2: 0, ATTN: 128}

C_ID, C_IOTA, C_SAME, C_HM4, C_HM8, C_TM, C_HX4, C_HX8, C_HZ, C_SZ4, C_SM4, C_SD, C_SZ8, C_ONE, C_END = (
    0, 128, 256, 384, 388, 396, 412, 540, 668, 676, 804, 932, 1060, 1188, 1189)
(V_AS1, V_AD1, V_B1, V_AS2, V_AD2, V_B2, V_BL, V_BR, V_ATT, V_BO, V_GW, V_GB, V_GM) = range(13)
(W_1, W_1T, W_2, W_2T, W_G, W_L, W_R, W_K, W_V, W_Q, W_O) = range(11)
R_G, R_LR, R_KVQ, R_O, R_END = 0, 128, 384, 768, 896


class Signal:

    def __init__(self, sem, totals):
        self.sem, self.totals = sem, totals

    def at(self, phase, n):
        return sum(self.totals.get(q, 0) for q in range(phase)) + n


def some(n):
    return not isinstance(n, int) or n > 0


class Group:

    def __init__(self, g, par, half):
        self.g, self.par, self.half = g, par, half


def each_group(eng, body, tail=None):
    zero, one = Group(0, 0, 0), Group(1, 1, 0)
    body(zero, None)
    body(one, zero)
    with eng.Fori(1, GROUPS // 2) as it:
        even, odd = Group(it * 2, 0, it), Group(it * 2 + 1, 1, it)
        body(even, Group(it * 2 - 1, 1, it - 1))
        body(odd, even)
    if tail is not None:
        tail(Group(GROUPS - 1, 1, GROUPS // 2 - 1))


def build(nc, x_in, src_idx, dst_tile, dst_first, dst_last, dst_last_prev, dst_flat, edge_attr, edge_attr_t,
          edge_weight, weights, w_edge, vectors, bias_rows, consts, out):
    with ExitStack() as ctx:
        def sb(name, shape, dt=F32):
            return ctx.enter_context(nc.sbuf_tensor(name, shape, dt))

        def sem(name):
            return ctx.enter_context(nc.semaphore(name))

        def dram(name, shape):
            return nc.dram_tensor(name, shape, F32, kind="Internal").ap()

        gtab = {p: dram(f"gather_table{p}", (NODES, ROWF[p])) for p in ROWF}
        wtab = {p: dram(f"window_table{p}", (TROWS, WINF[p])) for p in WINF}

        x = sb("x", [P, NI, D])
        hT = sb("hT", [P, NCOL])
        acc = sb("acc", [P, ACOL])
        zacc = sb("zacc", [9, ACOL])
        eacc = sb("eacc", [ED, ACOL])
        vring = sb("gathered_rows", [P, 2 * GT, VROW])
        oh = sb("one_hot", [P, 2 * GT, P])
        ohT = sb("one_hot_t", [P, 2, 4 * P])
        tq_sb = sb("edge_features", [P, 2, 4 * P])
        win = sb("window_rows", [P, 8, D])
        ering = sb("edge_attr_ring", [P, 2, GT * ED])
        msg = sb("messages", [P, 2, 2, D])
        wm = sb("weights_and_max", [P, 2, GT, 9])
        s_sb = sb("scores", [P, P])
        s_tmp = sb("scores_sum", [P, P])
        fwd = sb("running_max", [P, P])
        bwd = sb("tile_max", [P, P])
        shift = sb("shift", [P, P])
        diff = sb("diff", [P, P + 1])
        wexp = sb("chunk_weights", [P, P + 1])
        mend = sb("end_max", [P, P])
        resc = sb("rescale", [P, 2, GT])
        rdiag = sb("rescale_diag", [P, GT])
        start_pen = sb("start_pen", [P, ACOL], BF16)
        end_pen = sb("end_pen_reversed", [P, ACOL], BF16)
        first_pen = sb("first_pen", [P, ACOL], BF16)
        is_end = sb("is_end", [P, ACOL], BF16)
        cin = sb("carry_in", [1, 8, GT + 1])
        crow = sb("carry_row", [1, 8, GT + 1])
        cshift = sb("carry_shifted", [1, 8 * GT])
        row_pen = sb("row_pen", [1, GROUPS, 8, GT + 1], BF16)
        cont_pen = sb("cont_pen", [1, TILES])
        last_i = sb("dst_last", [1, 2, TILES], I32)
        idx_all = sb("src_index", [P, TILES], I32)
        idx = sb("src_index_ring", [P, 2, GT], I32)
        dfirst = sb("dst_first", [1, TILES], I32)
        drel = sb("dst_relative", [P, TILES])
        ew = sb("edge_weight", [P, TILES])
        cst = sb("constants", [P, C_END])
        wts = sb("weights", [P, 11, D])
        we = sb("w_edge", [ED, D])
        vec = sb("vectors", [P, 13])
        brow = sb("bias_rows", [P, R_END])
        gat_cols = sb("gat_cols", [P, 2, 8])
        gat_rep = sb("gat_same_head", [P, 2, D])
        gat_w = sb("gat_w", [P, 2, 136])
        gat_wrep = sb("gat_w_loop", [P, 2, D])
        att_rep = sb("att_same_head", [P, 2, D])
        att_col = sb("att_cols", [P, 2, 4])
        blr = sb("bl_plus_br", [P, 2])
        stat = sb("ln_stat", [P, NI, 6])
        mv = sb("ln_mean_var", [P, NI, 2])
        lnv = sb("ln_vectors", [P, 4, NI])
        norm = sb("norm", [P, 2, NI])
        gn = sb("graph_norm", [P, 8])

        hn = oh[0:NP, 0:8, :]
        oh_flat = oh[:, :, :].rearrange("p a b -> p (a b)").bitcast(I32)
        dtile, dfirst_b = oh_flat[:, 8 * P:8 * P + TILES], oh_flat[:, 8 * P + TILES:8 * P + 2 * TILES]
        kt_sb = ering[:, :, 4 * P:8 * P]
        tab = vring[0:NP, 0:16, :].rearrange("p a b -> p (a b)")[:, 0:2 * TC * 384].rearrange(
            "p (s i f) -> p s i f", s=2, i=TC)
        vflat = vring[:, :, :].rearrange("p a b -> p (a b)")

        d_cur = acc[:, :].bitcast(I32).rearrange("p (g e) -> p g e", e=P)
        d_prev = vflat[:, 0:ACOL].bitcast(I32).rearrange("p (g e) -> p g e", e=P)
        d_next = vflat[:, ACOL:2 * ACOL].bitcast(I32).rearrange("p (g e) -> p g e", e=P)

        def temp(par, n, w=1):
            at = (par * 8 + n) * CH
            return vflat[:, at:at + w * CH]

        ident = cst[:, C_ID:C_ID + P]
        tq_flat = tq_sb[:, :, :].rearrange("p s e -> p (s e)")
        end_pen_r = end_pen[:, :].rearrange("p (g e) -> p g e", e=P)[:, :, ::-1]
        psum = [ctx.enter_context(nc.psum_tensor(f"bank{b}", [P, 512], F32)) for b in range(8)]
        b_oht, b_feat, b_keys, b_small, b_sum0, b_sum1, b_e, b_w = psum
        b_sum = (b_sum0, b_sum1)
        p_score, p_chunk, p_last = b_small[:, 0:128], b_small[:, 128:256], b_small[0:1, 256:384]
        p_carry, p_resc, p_rescz = b_small[:, 384:385], b_small[:, 392:408], b_small[0:8, 408:424]
        p_wt, p_mt = b_w[:, 0:128], b_w[:, 128:192]

        ALL = range(5)
        per_group = lambda n, phases=SOFTMAX: {q: n * GROUPS for q in phases}

        def signal(name, totals):
            return Signal(sem(name), totals)

        loaded = sem("inputs_loaded")
        setup = sem("dve_setup")
        waited = sem("waited_apart")
        link_sem = sem("dve_chain")
        prepared = sem("weights_prepared")
        gat_mm = sem("gat_weight_products")
        zeroed = sem("window_pads_stored")
        ln_stats = signal("ln_statistics", {q: 1 for q in LN_OF})
        ln_var = signal("ln_variance", {q: 1 for q in LN_OF})
        ln_std = signal("ln_deviation", {q: 1 for q in LN_OF})
        hn_made = signal("normalized", {q: NI for q in LN_OF})
        hn_turned = signal("normalized_transposed", {q: NB for q in LN_OF})
        ht_made = signal("hT_written", {q: NB for q in LN_OF})
        tab_mm = signal("table_product", {q: NI for q in ALL})
        tab_made = signal("table_rows", {q: NI for q in ALL})
        tab_stored = [sem(f"table_stored{s}") for s in range(2)]
        deg_turned = signal("degree_transposed", {GCN: 1})
        deg_made = signal("degree", {GCN: 2})
        deg_root = signal("degree_root", {GCN: 1})
        idx_copied = signal("src_index_copied", {q: GROUPS for q in ALL})
        rows_in = [[signal(f"rows_gathered{a}{b}", {q: 64 * GROUPS // 2 for q in ALL}) for b in range(4)]
                   for a in range(2)]
        win_in = [signal(f"window_loaded{s}", per_group(32)) for s in range(8)]
        ea_in = [signal(f"edge_attr_loaded{s}", {GCN: 16 * GROUPS // 2, GATV2: 32 * GROUPS}) for s in range(2)]
        oh_made = signal("one_hot_made", {**per_group(16), GCN: 32 * GROUPS})
        oh_turned = signal("one_hot_transposed", per_group(4))
        oh_copied = signal("one_hot_t_copied", per_group(4))
        feat_mm = signal("edge_features_product", per_group(4))
        feat_act = signal("edge_features_copied", per_group(4, (GATV2, ATTN)))
        feat_mul = signal("query_times_key", per_group(4, (ATTN,)))
        score_mm = signal("score_product", per_group(4, (GATV2, ATTN)))
        score_sum = signal("score_summed", per_group(1, (GAT1, GAT2)))
        score_out = signal("scores_copied", per_group(1))
        chunk_in = signal("scores_transposed", per_group(1))
        fwd_made = signal("running_max_made", per_group(1))
        bwd_made = signal("tile_max_made", per_group(1))
        last_turned = signal("last_max_transposed", per_group(1))
        last_copied = signal("last_max_copied", per_group(1))
        carry_made = signal("carry_made", per_group(1))
        carry_out = signal("carry_shifted_made", per_group(2))
        carry_turned = signal("carry_transposed", per_group(1))
        shift_made = signal("shift_made", per_group(1))
        diff_made = signal("diff_made", per_group(2))
        mend_made = signal("end_max_made", per_group(1, (GAT1, GAT2, GATV2)))
        wexp_made = signal("chunk_weights_made", per_group(1))
        w_turned = signal("weights_transposed", per_group(1))
        wm_copied = signal("weights_copied", {GAT1: 2 * GROUPS, GAT2: 2 * GROUPS, GATV2: 2 * GROUPS, ATTN: GROUPS})
        rdiag_made = signal("rescale_diag_made", per_group(1))
        resc_mm = signal("rescale_product", per_group(1))
        resc_copied = signal("rescale_copied", per_group(2))
        msg_made = signal("messages_made", {**per_group(8)})
        agg_mm = signal("aggregate_product", {q: 8 * GROUPS for q in ALL})
        added = signal("accumulated", {**per_group(64), GCN: 32 * GROUPS})
        cleared = signal("accumulators_cleared", {GAT1: 3, GAT2: 3, GCN: 2, GATV2: 3, ATTN: 3})
        fin_deg = signal("loop_degree_product", {GATV2: NCH})
        fin_attr = signal("loop_attr_made", {GATV2: NCH})
        fin_feat = signal("loop_features_product", {GATV2: NCH})
        fin_leaky = signal("loop_features_leaky", {GATV2: NCH})
        fin_mm = signal("node_products", {GAT1: NCH, GAT2: NCH, GATV2: NCH, ATTN: NCH})
        fin_loop = signal("loop_score", {GAT1: NCH, GAT2: NCH, GATV2: NCH})
        fin_diff = signal("node_diff", {GAT1: NCH, GAT2: NCH, GATV2: NCH})
        fin_exp = signal("node_exp", {GAT1: NCH, GAT2: NCH, GATV2: NCH})
        fin_sum = signal("node_sum", {GAT1: NCH, GAT2: NCH, GATV2: NCH, ATTN: NCH})
        fin_out = signal("node_out", {GAT1: NCH, GAT2: NCH, GATV2: NCH})
        gn_mean = signal("graph_mean", {GATV2: 1})
        gn_sq = signal("graph_square_sum", {GATV2: 1})
        gn_var = signal("graph_variance", {GATV2: 1})
        gn_std = signal("graph_deviation", {GATV2: 1})
        gn_scale = signal("graph_scale", {GATV2: 1})
        gn_out = signal("graph_norm_out", {GATV2: 1})
        res_turned = signal("residual_transposed", {GAT2: NB, GCN: NB, GATV2: NB, ATTN: NB})
        res_added = signal("residual_added", {GAT2: NB, GCN: NB, GATV2: NB, ATTN: NB})
        out_stored = sem("out_stored")

        LOADS = 13 + 3 * 8
        def tab_count(phase, chunk, slot):
            n = 0
            for q in range(phase + 1):
                for c in range(TC if q < phase else chunk + 1):
                    if c % 2 == slot:
                        n += 16 * (2 if q in WINF else 1)
            return n

        def slot_count(phase, c):
            if c >= 2:
                return tab_count(phase, c - 2, c % 2)
            return tab_count(phase - 1, TC - 1, c % 2) if phase > 0 else 0

        def batch(b):
            return range(TB * b, min(TB * b + TB, NI))

        def chunk(c):
            return slice(c * CH, (c + 1) * CH)

        block = ctx.enter_context(nc.Block())

        @block.sync
        def _(sp):
            sp.dma_start(x[0:NP, :, :], x_in.rearrange("(p i) f -> p i f", i=NI)).then_inc(loaded, 16)
            sp.dma_start(cst[:, :], consts[:, :]).then_inc(loaded, 16)
            sp.dma_start(wts[:, :, :], weights.rearrange("p (n f) -> p n f", n=11)).then_inc(loaded, 16)
            sp.dma_start(vec[:, :], vectors[:, :]).then_inc(loaded, 16)
            sp.dma_start(idx_all[:, :], src_idx[:, :]).then_inc(loaded, 16)
            sp.dma_start(dtile[:, :], dst_tile[:, :]).then_inc(loaded, 16)
            sp.dma_start(dfirst_b[:, :], dst_first[0:1, :].to_broadcast([P, TILES])).then_inc(loaded, 16)
            sp.dma_start(dfirst[:, :], dst_first[:, :]).then_inc(loaded, 16)
            sp.dma_start(last_i[:, 0, :], dst_last[:, :]).then_inc(loaded, 16)
            sp.dma_start(last_i[:, 1, :], dst_last_prev[:, :]).then_inc(loaded, 16)
            sp.dma_start(we[:, :], w_edge[:, :]).then_inc(loaded, 16)
            sp.dma_start(brow[:, :], bias_rows[0:1, :].to_broadcast([P, R_END])).then_inc(loaded, 16)
            sp.dma_start(ew[:, :], edge_weight[:, :]).then_inc(loaded, 16)
            for d, off in ((d_cur, 1), (d_prev, 0), (d_next, 2)):
                by_chunk = dst_flat[off:off + EPAD].rearrange("(g t e) -> t g e", t=GT, e=P)
                for h in range(8):
                    sp.dma_start(d[GT * h:GT * (h + 1), :, :], by_chunk).then_inc(loaded, 16)
            sp.wait_ge(setup, 1)
            for q in WINF:
                sp.dma_start(wtab[q][NODES:TROWS, :], s_tmp[:, 0:WINF[q]]).then_inc(zeroed, 16)
            sp.wait_ge(zeroed, 16 * len(WINF))

            def store_tables(q):
                for c in range(TC):
                    s = c % 2
                    sp.wait_ge(tab_made.sem, tab_made.at(q, TC * (c + 1)))
                    g = gtab[q][0:NODES, :].rearrange("(p i) f -> p i f", i=NI)[:, TC * c:TC * (c + 1), :]
                    sp.dma_start(g, tab[:, s, :, 0:ROWF[q]]).then_inc(tab_stored[s], 16)
                    if q in WINF:
                        w = wtab[q][0:NODES, :].rearrange("(p i) f -> p i f", i=NI)[:, TC * c:TC * (c + 1), :]
                        sp.dma_start(w, tab[:, s, :, ROWF[q]:TF[q]]).then_inc(tab_stored[s], 16)

            def load_windows(q):
                sp.wait_ge(tab_stored[0], tab_count(q, TC - 1, 0))
                sp.wait_ge(tab_stored[1], tab_count(q, TC - 1, 1))

                def body(gr, before):
                    for t in range(4):
                        if some(gr.g * 4 + t - 1):
                            sp.wait_ge(feat_mm.sem, feat_mm.at(q, gr.g * 4 + t - 1))
                        if q == GATV2:
                            e0 = gr.g * (GT * P) + t * 4 * P
                            sp.dma_start(ering[0:ED, t % 2, 0:4 * P],
                                         edge_attr_t[:, bass.ds(e0, 4 * P)]).then_inc(ea_in[t % 2].sem, 16)
                        for j in range(4):
                            k = 4 * t + j
                            d0 = sp.value_load(dfirst[0:1, bass.ds(gr.g * GT + k, 1)], min_val=0, max_val=NODES)
                            sp.dma_start(win[:, k % 8, 0:WINF[q]],
                                         wtab[q][bass.ds(d0, P), :]).then_inc(win_in[k % 8].sem, 16)

                each_group(sp, body)

            def load_edge_attr(q):
                def body(gr, before):
                    if some(gr.g * 8 - 8):
                        sp.wait_ge(agg_mm.sem, agg_mm.at(q, gr.g * 8 - 8))
                    v = edge_attr[:, bass.ds(gr.g * (GT * ED), GT * ED)]
                    sp.dma_start(ering[:, gr.par, :], v).then_inc(ea_in[gr.par].sem, 16)

                each_group(sp, body)

            for q in ALL:
                store_tables(q)
                if q in WINF:
                    load_windows(q)
                else:
                    load_edge_attr(q)
            sp.wait_ge(res_added.sem, res_added.at(ATTN, NB))
            sp.dma_start(out.rearrange("(p i) f -> p i f", i=NI), x[0:NP, :, :]).then_inc(out_stored, 16)
            sp.wait_ge(out_stored, 16)

        @block.gpsimd
        def _(pool):
            pool.wait_ge(loaded, 16 * LOADS)
            for q in ALL:
                pool.wait_ge(tab_stored[0], tab_count(q, TC - 1, 0))
                pool.wait_ge(tab_stored[1], tab_count(q, TC - 1, 1))

                def body(gr, before):
                    for b in range(4):
                        if some(gr.half * 64):
                            pool.wait_ge(rows_in[gr.par][b].sem, rows_in[gr.par][b].at(q, gr.half * 64))
                    if some(gr.g):
                        pool.wait_ge(idx_copied.sem, idx_copied.at(q, gr.g))
                    nc.gpsimd.tensor_copy(idx[:, gr.par, :], idx_all[:, bass.ds(gr.g * GT, GT)]).then_inc(
                        idx_copied.sem, 1)
                    pool.wait_ge(idx_copied.sem, idx_copied.at(q, gr.g + 1))
                    for k in range(GT):
                        if k % 2 == 0:
                            used = agg_mm if q == GCN else msg_made
                            if some(gr.g * 8 - 16 + k // 2 + 1):
                                pool.wait_ge(used.sem, used.at(q, gr.g * 8 - 16 + k // 2 + 1))
                                pool.sem_inc(waited, 1)
                        pool.indirect_dma_start(
                            vring[:, gr.par * GT + k, 0:ROWF[q]], None, gtab[q][:, :],
                            bass.IndirectOffsetOnAxis(ap=idx[:, gr.par, k:k + 1], axis=0),
                        ).then_inc(rows_in[gr.par][k // 4].sem, 16)

                each_group(pool, body)

        @block.tensor
        def _(pe):
            mm, tr = nc.tensor.matmul, nc.tensor.transpose

            def wt(n):
                return wts[:, n, :]

            pe.wait_ge(loaded, 16 * LOADS)
            pe.wait_ge(prepared, 1)
            for n, w in ((0, W_1T), (1, W_2T)):
                mm(b_oht[:, 256 * n:256 * n + 8], wt(w), gat_cols[:, n, :], start=True, stop=True)
                mm(b_oht[:, 256 * n + 128:256 * n + 256], wt(w), gat_rep[:, n, :], start=True,
                   stop=True).then_inc(gat_mm, 1)

            def turn_hidden(q):
                for b in range(NB):
                    pe.wait_ge(hn_made.sem, hn_made.at(q, batch(b)[-1] + 1))
                    if some(b - 1):
                        pe.wait_ge(ht_made.sem, ht_made.at(q, b - 1))
                    bank = (b_oht, b_feat)[b % 2]
                    for j, i in enumerate(batch(b)):
                        last = tr(bank[:, j * NP:(j + 1) * NP], hn[:, i % 8, :], ident[0:NP, 0:NP])
                    last.then_inc(hn_turned.sem, 1)

            def table(q):
                rhs = {GAT1: gat_w[:, 0, :], GAT2: gat_w[:, 1, :], GCN: wt(W_G),
                       GATV2: wts[:, W_L:W_R + 1, :].rearrange("p n f -> p (n f)"),
                       ATTN: wts[:, W_K:W_Q + 1, :].rearrange("p n f -> p (n f)")}[q]
                if q == GAT2:
                    pe.wait_ge(fin_out.sem, fin_out.at(GAT1, NCH))
                else:
                    pe.wait_ge(ht_made.sem, ht_made.at(q, NB))
                if q == GAT1:
                    pe.wait_ge(prepared, 2)
                for i in range(NI):
                    if some(i - 1):
                        pe.wait_ge(tab_made.sem, tab_made.at(q, i - 1))
                    bank = (b_keys, b_e)[i % 2]
                    mm(bank[0:NP, 0:TF[q]], hT[:, i:NODES:NI], rhs, start=True, stop=True).then_inc(tab_mm.sem, 1)

            def softmax_pass(q):
                H = HEADS[q]
                TH = H * GT

                def turn_one_hot(gr, t):
                    pe.wait_ge(oh_made.sem, oh_made.at(q, gr.g * GT + 4 * t + 4))
                    if some(gr.g * 4 + t):
                        pe.wait_ge(oh_copied.sem, oh_copied.at(q, gr.g * 4 + t))
                    for j in range(4):
                        last = tr(b_oht[:, j * P:(j + 1) * P], oh[:, gr.par * GT + 4 * t + j, :], ident)
                    last.then_inc(oh_turned.sem, 1)

                def edge_features(gr, t):
                    pe.wait_ge(oh_copied.sem, oh_copied.at(q, gr.g * 4 + t + 1))
                    if q in (GATV2, ATTN):
                        pe.wait_ge(rows_in[gr.par][t].sem, rows_in[gr.par][t].at(q, gr.half * 64 + 64))
                    if q == GATV2:
                        pe.wait_ge(ea_in[t % 2].sem, ea_in[t % 2].at(q, gr.g * 32 + 16 * (t // 2) + 16))
                        if some(gr.g * 4 + t):
                            pe.wait_ge(feat_act.sem, feat_act.at(q, gr.g * 4 + t))
                    if q == ATTN:
                        if some(gr.g * 4 + t):
                            pe.wait_ge(feat_mul.sem, feat_mul.at(q, gr.g * 4 + t))
                    if q in (GAT1, GAT2) and t == 0:
                        if some(gr.g):
                            pe.wait_ge(score_sum.sem, score_sum.at(q, gr.g))
                        if some(gr.g * 2):
                            pe.wait_ge(resc_copied.sem, resc_copied.at(q, gr.g * 2))
                    for j in range(4):
                        k = 4 * t + j
                        rows = vring[:, gr.par * GT + k, 0:D]
                        pe.wait_ge(win_in[k % 8].sem, win_in[k % 8].at(q, gr.g * 32 + 16 * (k // 8) + 16))
                        o = ohT[:, t % 2, j * P:(j + 1) * P]
                        f = b_feat[:, j * P:(j + 1) * P]
                        if q in (GAT1, GAT2):
                            last = mm(p_score[:, 4 * k:4 * k + 4], o, win[:, k % 8, 0:4], start=True, stop=True)
                        elif q == GATV2:
                            mm(f, rows, ident, start=True, stop=False)
                            mm(f, win[:, k % 8, :], o, start=False, stop=False)
                            last = mm(f, we[:, :], ering[0:ED, t % 2, j * P:(j + 1) * P], start=False, stop=True)
                        else:
                            tr(b_keys[:, j * P:(j + 1) * P], rows, ident)
                            last = mm(f, win[:, k % 8, :], o, start=True, stop=True)
                    last.then_inc(feat_mm.sem, 1)

                def scores(gr, t):
                    if q == GATV2:
                        pe.wait_ge(feat_act.sem, feat_act.at(q, gr.g * 4 + t + 1))
                    else:
                        pe.wait_ge(feat_mul.sem, feat_mul.at(q, gr.g * 4 + t + 1))
                    if t == 0:
                        if some(gr.g):
                            pe.wait_ge(score_out.sem, score_out.at(q, gr.g))
                        if some(gr.g * 2):
                            pe.wait_ge(resc_copied.sem, resc_copied.at(q, gr.g * 2))
                    for j in range(4):
                        k = 4 * t + j
                        o, e = p_score[:, H * k:H * k + H], slice(j * P, (j + 1) * P)
                        if q == GATV2:
                            mm(o, tq_sb[:, t % 2, e], att_col[:, 0, :], start=True, stop=False)
                            last = mm(o, kt_sb[:, t % 2, e], att_col[:, 1, :], start=False, stop=True)
                        else:
                            last = mm(o, tq_sb[:, t % 2, e], cst[:, C_HM8:C_HM8 + 8], start=True, stop=True)
                    last.then_inc(score_mm.sem, 1)

                def aggregate(gr, p):
                    pe.wait_ge(msg_made.sem, msg_made.at(q, gr.g * 8 + p + 1))
                    pe.wait_ge(wm_copied.sem, wm_copied.at(q, (gr.g + 1) * (1 if q == ATTN else 2)))
                    if some(gr.g * 64 + 8 * (p - 1)):
                        pe.wait_ge(added.sem, added.at(q, gr.g * 64 + 8 * (p - 1)))
                    Z = 8 if q == ATTN else 9
                    for j in range(2):
                        k = 2 * p + j
                        o = oh[:, gr.par * GT + k, :]
                        mm(b_sum[p % 2][:, j * P:(j + 1) * P], msg[:, p % 2, j, :], o, start=True, stop=True)
                        last = mm(b_sum[p % 2][0:Z, (2 + j) * P:(3 + j) * P], wm[:, gr.par, k, 0:Z], o, start=True, stop=True)
                    last.then_inc(agg_mm.sem, 1)

                def softmax(gr):
                    pe.wait_ge(score_out.sem, score_out.at(q, gr.g + 1))
                    pe.sem_inc(waited, 1)
                    tr(p_chunk[0:TH, :], s_sb[:, 0:TH], ident).then_inc(chunk_in.sem, 1)
                    pe.wait_ge(fwd_made.sem, fwd_made.at(q, gr.g + 1))
                    pe.sem_inc(waited, 1)
                    tr(p_last[:, 0:TH], fwd[0:TH, P - 1:P], ident[0:TH, 0:TH]).then_inc(last_turned.sem, 1)
                    pe.wait_ge(carry_out.sem, carry_out.at(q, gr.g * 2 + 1))
                    pe.sem_inc(waited, 1)
                    tr(p_carry[0:TH, :], cshift[:, 0:TH], ident[0:1, 0:1]).then_inc(carry_turned.sem, 1)
                    if q != ATTN:
                        pe.wait_ge(mend_made.sem, mend_made.at(q, gr.g + 1))
                        pe.sem_inc(waited, 1)
                        tr(p_mt, mend[0:TH, :], ident[0:TH, 0:TH])
                    pe.wait_ge(wexp_made.sem, wexp_made.at(q, gr.g + 1))
                    if some(gr.g * 8):
                        pe.wait_ge(msg_made.sem, msg_made.at(q, gr.g * 8))
                        pe.sem_inc(waited, 1)
                    tr(p_wt[:, 0:TH], wexp[0:TH, 0:P], ident[0:TH, 0:TH]).then_inc(w_turned.sem, 1)
                    pe.wait_ge(rdiag_made.sem, rdiag_made.at(q, gr.g + 1))
                    hx = C_HX8 if q == ATTN else C_HX4
                    mm(p_resc, cst[0:TH, hx:hx + P], rdiag[0:TH, :], start=True, stop=True)
                    mm(p_rescz[0:H, :], cst[0:TH, C_HZ:C_HZ + H], rdiag[0:TH, :], start=True,
                       stop=True).then_inc(resc_mm.sem, 1)

                def body(gr, before):
                    for t in range(4):
                        turn_one_hot(gr, t)
                        if before is not None:
                            aggregate(before, 2 * t)
                            aggregate(before, 2 * t + 1)
                        edge_features(gr, t)
                        if t > 0 and q in (GATV2, ATTN):
                            scores(gr, t - 1)
                    if q in (GATV2, ATTN):
                        scores(gr, 3)
                    softmax(gr)

                def tail(gr):
                    for p in range(8):
                        aggregate(gr, p)

                each_group(pe, body, tail)

            def gcn_pass(q):
                def body(gr, before):
                    pe.wait_ge(ea_in[gr.par].sem, ea_in[gr.par].at(q, gr.half * 16 + 16))
                    for p in range(8):
                        if p % 2 == 0:
                            pe.wait_ge(rows_in[gr.par][p // 2].sem, rows_in[gr.par][p // 2].at(q, gr.half * 64 + 64))
                        pe.wait_ge(oh_made.sem, oh_made.at(q, gr.g * 32 + 4 * p + 4))
                        if some(gr.g * 32 + 4 * (p - 1)):
                            pe.wait_ge(added.sem, added.at(q, gr.g * 32 + 4 * (p - 1)))
                        for j in range(2):
                            k = 2 * p + j
                            mm(b_sum[p % 2][:, j * P:(j + 1) * P], vring[:, gr.par * GT + k, 0:D], oh[:, gr.par * GT + k, :],
                               start=True, stop=True)
                            last = mm(b_sum[p % 2][0:ED, (2 + j) * P:(3 + j) * P], ering[:, gr.par, ED * k:ED * (k + 1)],
                                      ohT[:, p % 2, j * P:(j + 1) * P], start=True, stop=True)
                        last.then_inc(agg_mm.sem, 1)

                each_group(pe, body)

            def banks(c):
                return psum[0:4] if c % 2 == 0 else psum[4:8]

            def node_products(q):
                pe.wait_ge(added.sem, added.at(q, 64 * GROUPS))
                for c in range(NCH):
                    hb, sbk, zb, mb = (b[:, 0:CH] for b in banks(c))
                    if some(c - 1):
                        pe.wait_ge(fin_sum.sem, fin_sum.at(q, c - 1))
                    z = zacc[0:9, chunk(c)]
                    if q == GATV2:
                        mm(mb[0:ED, :], cst[0:9, C_SD:C_SD + ED], z, start=True, stop=True).then_inc(fin_deg.sem, 1)
                        mm(hb, wt(W_L), hT[:, chunk(c)], start=True, stop=True)
                        mm(sbk, wt(W_L), hT[:, chunk(c)], start=True, stop=False)
                        mm(sbk, wt(W_R), hT[:, chunk(c)], start=False, stop=False)
                        pe.wait_ge(fin_attr.sem, fin_attr.at(q, c + 1))
                        mm(sbk, we[:, :], eacc[:, chunk(c)], start=False, stop=True).then_inc(fin_feat.sem, 1)
                        pe.wait_ge(fin_leaky.sem, fin_leaky.at(q, c + 1))
                        mm(sbk, att_rep[:, 0, :], tq_flat[:, 0:CH], start=True, stop=False)
                        mm(sbk, att_rep[:, 1, :], kt_sb[:, 0, 0:CH], start=False, stop=True)
                    elif q != ATTN:
                        mm(hb, wt(W_1 if q == GAT1 else W_2), hT[:, chunk(c)], start=True, stop=True)
                        mm(sbk, gat_wrep[:, 0 if q == GAT1 else 1, :], hT[:, chunk(c)], start=True, stop=True)
                    if q == ATTN:
                        mm(zb, cst[0:8, C_SZ8:C_SZ8 + P], z[0:8, :], start=True, stop=True).then_inc(fin_mm.sem, 1)
                    else:
                        mm(zb, cst[0:9, C_SZ4:C_SZ4 + P], z, start=True, stop=True)
                        mm(mb, cst[0:9, C_SM4:C_SM4 + P], z, start=True, stop=True).then_inc(fin_mm.sem, 1)

            def turn_residual(q):
                if q == GAT2:
                    pe.wait_ge(fin_out.sem, fin_out.at(q, NCH))
                elif q == GCN:
                    pe.wait_ge(added.sem, added.at(q, 32 * GROUPS))
                elif q == GATV2:
                    pe.wait_ge(gn_out.sem, gn_out.at(q, 1))
                else:
                    pe.wait_ge(fin_sum.sem, fin_sum.at(q, NCH))
                for b in range(NB):
                    if some(b - 1):
                        pe.wait_ge(res_added.sem, res_added.at(q, b - 1))
                    bank = (b_oht, b_feat)[b % 2]
                    for j, i in enumerate(batch(b)):
                        o = bank[0:NP, j * D:(j + 1) * D]
                        if q == ATTN:
                            last = mm(o, acc[:, i:NODES:NI], wt(W_O), start=True, stop=True)
                        else:
                            last = tr(o, acc[:, i:NODES:NI], ident)
                    last.then_inc(res_turned.sem, 1)

            def degrees(q):
                for i in range(NI):
                    last = tr(b_w[0:NP, 9 * i:9 * i + 9], zacc[0:9, i:NODES:NI], ident[0:9, 0:9])
                last.then_inc(deg_turned.sem, 1)

            turn_hidden(GAT1)
            table(GAT1)
            softmax_pass(GAT1)
            node_products(GAT1)
            table(GAT2)
            softmax_pass(GAT2)
            node_products(GAT2)
            turn_residual(GAT2)
            degrees(GCN)
            turn_hidden(GCN)
            table(GCN)
            gcn_pass(GCN)
            turn_residual(GCN)
            turn_hidden(GATV2)
            table(GATV2)
            softmax_pass(GATV2)
            node_products(GATV2)
            turn_residual(GATV2)
            turn_hidden(ATTN)
            table(ATTN)
            softmax_pass(ATTN)
            node_products(ATTN)
            turn_residual(ATTN)

        @block.scalar
        def _(act):
            func = nc.scalar.activation
            act.wait_ge(loaded, 16 * LOADS)

            def normalize(q):
                act.wait_ge(ln_var.sem, ln_var.at(q, 1))
                func(lnv[0:NP, 1, :], lnv[0:NP, 0, :], ACT.Sqrt).then_inc(ln_std.sem, 1)
                act.wait_ge(ln_stats.sem, ln_stats.at(q, 1))
                for i in range(NI):
                    if some(i // TB - 1):
                        act.wait_ge(hn_turned.sem, hn_turned.at(q, i // TB - 1))
                    func(hn[:, i % 8, :], x[0:NP, i, :], ACT.Relu, bias=lnv[0:NP, 3, i:i + 1],
                         scale=lnv[0:NP, 2, i:i + 1]).then_inc(hn_made.sem, 1)

            def table(q):
                for i in range(NI):
                    if q in (GATV2, ATTN):
                        return
                    if i % TC == 0 and (q > 0 or i // TC >= 2):
                        if some(slot_count(q, i // TC)):
                            act.wait_ge(tab_stored[(i // TC) % 2], slot_count(q, i // TC))
                    act.wait_ge(tab_mm.sem, tab_mm.at(q, i + 1))
                    if i == 0 and q == GCN:
                        act.wait_ge(deg_made.sem, deg_made.at(q, 2))
                    bank = (b_keys, b_e)[i % 2]
                    o = tab[:, (i // TC) % 2, i % TC, 0:TF[q]]
                    if q == GCN:
                        func(o, bank[0:NP, 0:TF[q]], ACT.Copy, scale=norm[0:NP, 1, i:i + 1]).then_inc(tab_made.sem, 1)
                    else:
                        func(o, bank[0:NP, 0:TF[q]], ACT.Copy).then_inc(tab_made.sem, 1)

            def softmax_pass(q):
                H = HEADS[q]
                TH = H * GT

                def body(gr, before):
                    for t in range(4):
                        act.wait_ge(oh_turned.sem, oh_turned.at(q, gr.g * 4 + t + 1))
                        if some(gr.g * 4 + t - 1):
                            act.wait_ge(feat_mm.sem, feat_mm.at(q, gr.g * 4 + t - 1))
                        func(ohT[:, t % 2, :], b_oht[:, :], ACT.Copy).then_inc(oh_copied.sem, 1)
                        if q == GATV2:
                            act.wait_ge(feat_mm.sem, feat_mm.at(q, gr.g * 4 + t + 1))
                            if some(gr.g * 4 + t - 1):
                                act.wait_ge(score_mm.sem, score_mm.at(q, gr.g * 4 + t - 1))
                            func(tq_sb[:, t % 2, :], b_feat[:, :], ACT.Relu)
                            func(kt_sb[:, t % 2, :], b_feat[:, :], ACT.Relu, scale=-1.0).then_inc(feat_act.sem, 1)
                        if q == ATTN:
                            act.wait_ge(feat_mm.sem, feat_mm.at(q, gr.g * 4 + t + 1))
                            if some(gr.g * 4 + t - 1):
                                act.wait_ge(feat_mul.sem, feat_mul.at(q, gr.g * 4 + t - 1))
                            func(kt_sb[:, t % 2, :], b_keys[:, :], ACT.Copy).then_inc(feat_act.sem, 1)
                    if q in (GATV2, ATTN):
                        act.wait_ge(score_mm.sem, score_mm.at(q, gr.g * 4 + 4))
                        if some(gr.g):
                            act.wait_ge(chunk_in.sem, chunk_in.at(q, gr.g))
                        func(s_sb[:, 0:TH].rearrange("p (h k) -> p h k", k=GT),
                             p_score[:, 0:TH].rearrange("p (k h) -> p h k", h=H), ACT.Copy,
                             scale=0.25 if q == ATTN else 1.0).then_inc(score_out.sem, 1)
                    act.wait_ge(diff_made.sem, diff_made.at(q, gr.g * 2 + 2))
                    if some(gr.g):
                        act.wait_ge(resc_mm.sem, resc_mm.at(q, gr.g))
                    func(wexp[0:TH, :], diff[0:TH, :], ACT.Exp).then_inc(wexp_made.sem, 1)
                    act.wait_ge(w_turned.sem, w_turned.at(q, gr.g + 1))
                    if some(gr.g * 8 - 8):
                        act.wait_ge(agg_mm.sem, agg_mm.at(q, gr.g * 8 - 8))
                    func(wm[:, gr.par, :, 0:H], p_wt[:, 0:TH].rearrange("p (h k) -> p k h", k=GT),
                         ACT.Copy).then_inc(wm_copied.sem, 1)
                    if q != ATTN:
                        func(wm[:, gr.par, :, 4:8], p_mt.rearrange("p (h k) -> p k h", k=GT),
                             ACT.Copy).then_inc(wm_copied.sem, 1)

                    act.wait_ge(resc_mm.sem, resc_mm.at(q, gr.g + 1))
                    if some(gr.g * 64):
                        act.wait_ge(added.sem, added.at(q, gr.g * 64))
                    func(resc[:, 0, :], p_resc, ACT.Copy).then_inc(resc_copied.sem, 1)
                    func(resc[0:H, 1, :], p_rescz[0:H, :], ACT.Copy).then_inc(resc_copied.sem, 1)

                each_group(act, body)

            def node_domain(q):
                if q == ATTN:
                    return
                for c in range(NCH + 1):
                    if c < NCH:
                        par = c % 2
                        bank = (psum[1] if par == 0 else psum[5])[:, 0:CH]
                        if q == GATV2:
                            act.wait_ge(fin_feat.sem, fin_feat.at(q, c + 1))
                            func(tq_flat[:, 0:CH], bank, ACT.Relu, bias=blr[:, 0:1])
                            func(kt_sb[:, 0, 0:CH], bank, ACT.Relu, bias=blr[:, 1:2], scale=-1.0).then_inc(
                                fin_leaky.sem, 1)
                        act.wait_ge(fin_mm.sem, fin_mm.at(q, c + 1))
                        func(temp(par, 0), bank, ACT.Copy).then_inc(fin_loop.sem, 1)
                        act.wait_ge(fin_diff.sem, fin_diff.at(q, c + 1))
                        func(temp(par, 4, 2), temp(par, 2, 2), ACT.Exp).then_inc(fin_exp.sem, 1)
                    if c > 0:
                        e, par = c - 1, (c - 1) % 2
                        act.wait_ge(fin_sum.sem, fin_sum.at(q, e + 1))
                        if q == GAT1:
                            func(hT[:, chunk(e)], temp(par, 6), ACT.Relu, bias=vec[:, V_B1:V_B1 + 1]).then_inc(
                                fin_out.sem, 1)
                        else:
                            b = V_B2 if q == GAT2 else V_BO
                            func(acc[:, chunk(e)], temp(par, 6), ACT.Identity, bias=vec[:, b:b + 1]).then_inc(
                                fin_out.sem, 1)

            def graph_norm(q):
                act.wait_ge(gn_mean.sem, gn_mean.at(q, 1))
                func(vflat[:, 0:NODES], acc[:, 0:NODES], ACT.Square, bias=gn[:, 2:3],
                     accum_out=gn[:, 3:4]).then_inc(gn_sq.sem, 1)
                act.wait_ge(gn_var.sem, gn_var.at(q, 1))
                func(gn[:, 5:6], gn[:, 4:5], ACT.Sqrt).then_inc(gn_std.sem, 1)
                act.wait_ge(gn_scale.sem, gn_scale.at(q, 1))
                func(acc[:, 0:NODES], acc[:, 0:NODES], ACT.Relu, bias=gn[:, 7:8], scale=gn[:, 6:7]).then_inc(
                    gn_out.sem, 1)

            def degree_root(q):
                act.wait_ge(deg_made.sem, deg_made.at(q, 1))
                func(norm[0:NP, 1, :], norm[0:NP, 0, :], ACT.Sqrt).then_inc(deg_root.sem, 1)

            normalize(GAT1)
            table(GAT1)
            softmax_pass(GAT1)
            node_domain(GAT1)
            table(GAT2)
            softmax_pass(GAT2)
            node_domain(GAT2)
            degree_root(GCN)
            normalize(GCN)
            table(GCN)
            normalize(GATV2)
            softmax_pass(GATV2)
            node_domain(GATV2)
            graph_norm(GATV2)
            normalize(ATTN)
            softmax_pass(ATTN)

        @block.vector
        def _(dve):
            v = nc.vector
            chain = [0]

            def link(ins):
                chain[0] += 1
                ins.then_inc(link_sem, 1)
                dve.wait_ge(link_sem, chain[0])

            def wt_rep(n):
                return vec[:, n:n + 1]

            v.memset(s_tmp[:, :], 0.0).then_inc(setup, 1)
            dve.wait_ge(loaded, 16 * LOADS)
            for n, (a, b) in enumerate(((V_AS1, V_AD1), (V_AS2, V_AD2))):
                v.tensor_scalar(gat_cols[:, n, 0:4], cst[:, C_HM4:C_HM4 + 4], vec[:, a:a + 1], None, ALU.mult)
                v.tensor_scalar(gat_cols[:, n, 4:8], cst[:, C_HM4:C_HM4 + 4], vec[:, b:b + 1], None, ALU.mult)
                link(v.tensor_tensor(blr[:, 0:1], vec[:, a:a + 1], vec[:, b:b + 1], ALU.add))
                link(v.tensor_scalar(gat_rep[:, n, :], cst[:, C_SAME:C_SAME + P], blr[:, 0:1], None, ALU.mult))
            v.memset(wm[:, :, :, :], 1.0)
            v.memset(hT[:, NODES:NCOL], 0.0)
            link(v.tensor_tensor(blr[:, 0:1], vec[:, V_BL:V_BL + 1], vec[:, V_BR:V_BR + 1], ALU.add))
            v.tensor_scalar(blr[:, 1:2], blr[:, 0:1], -1.0, None, ALU.mult)
            for n, f in ((0, 1.0), (1, -NEG)):
                v.tensor_scalar(att_rep[:, n, :], cst[:, C_SAME:C_SAME + P], vec[:, V_ATT:V_ATT + 1], f,
                                ALU.mult, ALU.mult)
                last = v.tensor_scalar(att_col[:, n, :], cst[:, C_HM4:C_HM4 + 4], vec[:, V_ATT:V_ATT + 1], f,
                                       ALU.mult, ALU.mult)
            last.then_inc(prepared, 1)
            a3 = lambda ap: ap.rearrange("p (g e) -> p g e", e=P)
            v.tensor_tensor(a3(start_pen[:, :]), d_cur, d_prev, ALU.not_equal)
            v.tensor_tensor(a3(is_end[:, :]), d_cur, d_next, ALU.not_equal)
            v.tensor_tensor(a3(first_pen[:, :]), d_cur, d_cur[:, :, 0:1].to_broadcast([P, GROUPS, P]),
                            ALU.not_equal)
            v.tensor_tensor(cont_pen[:, :], dfirst[:, :], last_i[:, 1, :], ALU.not_equal)
            v.tensor_tensor(drel[:, :], dtile[:, :], dfirst_b[:, :], ALU.subtract)
            v.memset(row_pen[:, :, :, :], -BIG)
            link(v.tensor_tensor(last_i[:, 0, :], last_i[:, 0, :], last_i[:, 1, :], ALU.not_equal))
            v.tensor_scalar(end_pen_r, a3(is_end[:, :]), -BIG, None, ALU.mult)
            v.tensor_scalar(start_pen[:, :], start_pen[:, :], -BIG, None, ALU.mult)
            v.tensor_scalar(first_pen[:, :], first_pen[:, :], -BIG, None, ALU.mult)
            v.tensor_scalar(cont_pen[:, :], cont_pen[:, :], -BIG, None, ALU.mult)
            for h in range(8):
                link(v.tensor_scalar(row_pen[:, :, h, 1:GT + 1],
                                     last_i[:, 0, :].rearrange("p (g t) -> p g t", t=GT), -BIG, None, ALU.mult))
            for n, w in ((0, W_1), (1, W_2)):
                dve.wait_ge(gat_mm, 2)
                v.tensor_copy(gat_w[:, n, 0:D], wts[:, w, :])
                v.tensor_copy(gat_w[:, n, D:D + 8], b_oht[:, 256 * n:256 * n + 8])
                last = v.tensor_copy(gat_wrep[:, n, :], b_oht[:, 256 * n + 128:256 * n + 256])
            last.then_inc(prepared, 1)

            def statistics(q):
                for i in range(NI):
                    last = v.bn_stats(stat[0:NP, i, :], x[0:NP, i, :])
                link(last)
                for i in range(NI):
                    last = v.bn_aggr(mv[0:NP, i, :], stat[0:NP, i, :])
                link(last)
                v.tensor_scalar(lnv[0:NP, 0, :], mv[0:NP, :, 1], EPS, None, ALU.add).then_inc(ln_var.sem, 1)
                dve.wait_ge(ln_std.sem, ln_std.at(q, 1))
                link(v.reciprocal(lnv[0:NP, 2, :], lnv[0:NP, 1, :]))
                v.scalar_tensor_tensor(out=lnv[0:NP, 3, :], in0=mv[0:NP, :, 0], scalar=-1.0, in1=lnv[0:NP, 2, :],
                                       op0=ALU.mult, op1=ALU.mult).then_inc(ln_stats.sem, 1)

            def hidden(q):
                cols = hT[:, 0:NODES].rearrange("f (p i) -> f i p", i=NI)
                for b in range(NB):
                    dve.wait_ge(hn_turned.sem, hn_turned.at(q, b + 1))
                    n = len(batch(b))
                    bank = (b_oht, b_feat)[b % 2]
                    v.tensor_copy(cols[:, TB * b:TB * b + n, :],
                                  bank[:, 0:n * NP].rearrange("f (i p) -> f i p", p=NP)).then_inc(ht_made.sem, 1)

            def table(q):
                lo, hi = (R_LR, R_KVQ) if q == GATV2 else (R_KVQ, R_O)
                for i in range(NI):
                    if i % TC == 0:
                        if some(slot_count(q, i // TC)):
                            dve.wait_ge(tab_stored[(i // TC) % 2], slot_count(q, i // TC))
                    dve.wait_ge(tab_mm.sem, tab_mm.at(q, i + 1))
                    bank = (b_keys, b_e)[i % 2]
                    v.tensor_tensor(tab[:, (i // TC) % 2, i % TC, 0:TF[q]], bank[0:NP, 0:TF[q]],
                                    brow[0:NP, lo:hi], ALU.add).then_inc(tab_made.sem, 1)

            def clear(q):
                v.memset(acc[:, :], 0.0).then_inc(cleared.sem, 1)
                if q == GCN:
                    v.memset(eacc[:, :], 0.0).then_inc(cleared.sem, 1)
                else:
                    v.memset(zacc[:, :], 0.0).then_inc(cleared.sem, 1)
                    v.memset(cin[:, :, :], -BIG).then_inc(cleared.sem, 1)
                dve.wait_ge(cleared.sem, cleared.at(q, 2 if q == GCN else 3))

            regs = [dve.alloc_register(f"window{k}") for k in range(GT)]

            def windows(gr):
                dve.load(regs, dfirst[0:1, bass.ds(gr.g * GT, GT)])
                return [dve.snap(r, min_val=0, max_val=NODES) for r in regs]

            def one_hot(gr, k, out, weight=None):
                t = gr.g * GT + k
                if weight is None:
                    return v.tensor_scalar(out, cst[:, C_IOTA:C_IOTA + P], drel[:, bass.ds(t, 1)], None, ALU.is_equal)
                return v.tensor_scalar(out, cst[:, C_IOTA:C_IOTA + P], drel[:, bass.ds(t, 1)],
                                       weight[:, bass.ds(t, 1)], ALU.is_equal, ALU.mult)

            def softmax_pass(q):
                H = HEADS[q]
                TH = H * GT
                off = VOFF[q]

                def hk(ap):
                    return ap.rearrange("p (h k) -> p h k", k=GT)

                def messages(gr, p):
                    rows = vring[:, gr.par * GT + 2 * p:gr.par * GT + 2 * p + 2, off:off + D]
                    w = p_wt[:, 0:TH].rearrange("p (h k) -> p k h", k=GT)[:, 2 * p:2 * p + 2, :]
                    if q == ATTN:
                        rows = rows.rearrange("e k (d h) -> e k d h", h=H)
                        w = w.unsqueeze(2).to_broadcast([P, 2, D // H, H])
                        o = msg[:, p % 2, :, :].rearrange("e k (d h) -> e k d h", h=H)
                    else:
                        rows = rows.rearrange("e k (h c) -> e k h c", h=H)
                        w = w.unsqueeze(3).to_broadcast([P, 2, H, D // H])
                        o = msg[:, p % 2, :, :].rearrange("e k (h c) -> e k h c", h=H)
                    dve.wait_ge(wm_copied.sem, wm_copied.at(q, (gr.g + 1) * (1 if q == ATTN else 2)))
                    if p % 2 == 0:
                        dve.wait_ge(rows_in[gr.par][p // 2].sem, rows_in[gr.par][p // 2].at(q, gr.half * 64 + 64))
                    if some(gr.g * 8 + p - 1):
                        dve.wait_ge(agg_mm.sem, agg_mm.at(q, gr.g * 8 + p - 1))
                    v.tensor_tensor(o, rows, w, ALU.mult).then_inc(msg_made.sem, 1)

                def accumulate(gr, p, starts):
                    dve.wait_ge(agg_mm.sem, agg_mm.at(q, gr.g * 8 + p + 1))
                    if p == 0:
                        dve.wait_ge(resc_copied.sem, resc_copied.at(q, gr.g * 2 + 2))
                    Z = 8 if q == ATTN else 9
                    for j in range(2):
                        k = 2 * p + j
                        n = gr.g * 64 + 4 * k
                        bank = b_sum[p % 2]
                        a0, z0 = acc[:, bass.ds(starts[k], 1)], zacc[0:H, bass.ds(starts[k], 1)]
                        aw, zw = acc[:, bass.ds(starts[k], P)], zacc[0:Z, bass.ds(starts[k], P)]
                        if some(n):
                            dve.wait_ge(added.sem, added.at(q, n))
                        v.tensor_tensor(a0, a0, resc[:, 0, k:k + 1], ALU.mult).then_inc(added.sem, 1)
                        v.tensor_tensor(z0, z0, resc[0:H, 1, k:k + 1], ALU.mult).then_inc(added.sem, 1)
                        dve.wait_ge(added.sem, added.at(q, n + 2))
                        v.tensor_tensor(aw, aw, bank[:, j * P:(j + 1) * P], ALU.add).then_inc(added.sem, 1)
                        v.tensor_tensor(zw, zw, bank[0:Z, (2 + j) * P:(3 + j) * P], ALU.add).then_inc(added.sem, 1)

                def query_times_key(gr, t):
                    dve.wait_ge(feat_act.sem, feat_act.at(q, gr.g * 4 + t + 1))
                    if some(gr.g * 4 + t - 1):
                        dve.wait_ge(score_mm.sem, score_mm.at(q, gr.g * 4 + t - 1))
                    v.tensor_tensor(tq_sb[:, t % 2, :], kt_sb[:, t % 2, :], b_feat[:, :], ALU.mult).then_inc(
                        feat_mul.sem, 1)

                def softmax(gr):
                    if q in (GAT1, GAT2):
                        dve.wait_ge(feat_mm.sem, feat_mm.at(q, gr.g * 4 + 4))
                        dve.wait_ge(rows_in[gr.par][3].sem, rows_in[gr.par][3].at(q, gr.half * 64 + 64))
                        for b in range(3):
                            dve.wait_ge(rows_in[gr.par][b].sem, rows_in[gr.par][b].at(q, gr.half * 64 + 64))
                        v.tensor_tensor(hk(s_tmp[:, 0:TH]), p_score[:, 0:TH].rearrange("p (k h) -> p h k", h=H),
                                        vring[:, gr.par * GT:(gr.par + 1) * GT, D:D + 4].rearrange("p k h -> p h k"),
                                        ALU.add).then_inc(score_sum.sem, 1)
                        dve.wait_ge(score_sum.sem, score_sum.at(q, gr.g + 1))
                        if some(gr.g):
                            dve.wait_ge(chunk_in.sem, chunk_in.at(q, gr.g))
                        v.scalar_tensor_tensor(out=s_sb[:, 0:TH], in0=s_tmp[:, 0:TH], scalar=NEG,
                                               in1=s_tmp[:, 0:TH], op0=ALU.mult, op1=ALU.max).then_inc(
                            score_out.sem, 1)
                    pen = bass.ds(gr.g * P, P)
                    dve.wait_ge(chunk_in.sem, chunk_in.at(q, gr.g + 1))
                    if some(gr.g):
                        dve.wait_ge(last_turned.sem, last_turned.at(q, gr.g))
                    v.tensor_tensor_scan(fwd[0:TH, :], start_pen[0:TH, pen], p_chunk[0:TH, :], -BIG,
                                         ALU.add, ALU.max).then_inc(fwd_made.sem, 1)
                    dve.wait_ge(fwd_made.sem, fwd_made.at(q, gr.g + 1))
                    v.tensor_tensor_scan(bwd[0:TH, ::-1], end_pen[0:TH, pen], fwd[0:TH, ::-1], -BIG,
                                         ALU.add, ALU.max).then_inc(bwd_made.sem, 1)
                    dve.wait_ge(last_turned.sem, last_turned.at(q, gr.g + 1))
                    if some(gr.g * 2):
                        dve.wait_ge(carry_out.sem, carry_out.at(q, gr.g * 2))
                    v.tensor_copy(cin[:, 0:H, 1:GT + 1], hk(p_last[:, 0:TH])).then_inc(last_copied.sem, 1)
                    dve.wait_ge(last_copied.sem, last_copied.at(q, gr.g + 1))
                    v.tensor_tensor_scan(crow[:, 0:H, :].rearrange("p h k -> p (h k)"),
                                         row_pen[:, bass.ds(gr.g, 1), 0:H, :].rearrange("p g h k -> p (g h k)"),
                                         cin[:, 0:H, :].rearrange("p h k -> p (h k)"), -BIG,
                                         ALU.add, ALU.max).then_inc(carry_made.sem, 1)
                    dve.wait_ge(carry_made.sem, carry_made.at(q, gr.g + 1))
                    if some(gr.g):
                        dve.wait_ge(carry_turned.sem, carry_turned.at(q, gr.g))
                    v.tensor_tensor(hk(cshift[:, 0:TH]), crow[:, 0:H, 0:GT],
                                    cont_pen[:, bass.ds(gr.g * GT, GT)].unsqueeze(1).to_broadcast([1, H, GT]),
                                    ALU.add).then_inc(carry_out.sem, 1)
                    v.tensor_copy(cin[:, 0:H, 0:1], crow[:, 0:H, GT:GT + 1]).then_inc(carry_out.sem, 1)
                    dve.wait_ge(carry_turned.sem, carry_turned.at(q, gr.g + 1))
                    dve.wait_ge(bwd_made.sem, bwd_made.at(q, gr.g + 1))
                    v.scalar_tensor_tensor(out=shift[0:TH, :], in0=first_pen[0:TH, pen], scalar=p_carry[0:TH, :],
                                           in1=bwd[0:TH, :], op0=ALU.add, op1=ALU.max).then_inc(shift_made.sem, 1)
                    dve.wait_ge(shift_made.sem, shift_made.at(q, gr.g + 1))
                    if some(gr.g):
                        dve.wait_ge(wexp_made.sem, wexp_made.at(q, gr.g))
                    v.tensor_tensor(diff[0:TH, 0:P], p_chunk[0:TH, :], shift[0:TH, :], ALU.subtract).then_inc(
                        diff_made.sem, 1)
                    v.tensor_tensor(diff[0:TH, P:P + 1], p_carry[0:TH, :], shift[0:TH, 0:1],
                                    ALU.subtract).then_inc(diff_made.sem, 1)
                    if q != ATTN:
                        if some(gr.g):
                            dve.wait_ge(w_turned.sem, w_turned.at(q, gr.g))
                        v.tensor_tensor(mend[0:TH, :], shift[0:TH, :], is_end[0:TH, pen], ALU.mult).then_inc(
                            mend_made.sem, 1)
                    dve.wait_ge(wexp_made.sem, wexp_made.at(q, gr.g + 1))
                    if some(gr.g):
                        dve.wait_ge(resc_mm.sem, resc_mm.at(q, gr.g))
                    v.tensor_scalar(rdiag[0:TH, :], cst[0:TH, C_TM:C_TM + GT], wexp[0:TH, P:P + 1], None,
                                    ALU.mult).then_inc(rdiag_made.sem, 1)

                def body(gr, before):
                    starts = windows(before) if before is not None else None
                    for t in range(4):
                        for k in range(4 * t, 4 * t + 4):
                            one_hot(gr, k, oh[:, gr.par * GT + k, :]).then_inc(oh_made.sem, 1)
                        if before is not None:
                            for p in (2 * t, 2 * t + 1):
                                messages(before, p)
                                if p > 0:
                                    accumulate(before, p - 1, starts)
                        if q == ATTN and t > 0:
                            query_times_key(gr, t - 1)
                    if before is not None:
                        accumulate(before, 7, starts)
                    if q == ATTN:
                        query_times_key(gr, 3)
                    softmax(gr)

                def tail(gr):
                    starts = windows(gr)
                    for p in range(8):
                        messages(gr, p)
                        if p > 0:
                            accumulate(gr, p - 1, starts)
                    accumulate(gr, 7, starts)

                each_group(dve, body, tail)
                dve.wait_ge(added.sem, added.at(q, 64 * GROUPS))

            def gcn_pass(q):
                def body(gr, before):
                    starts = windows(gr)

                    def accumulate(p):
                        dve.wait_ge(agg_mm.sem, agg_mm.at(q, gr.g * 8 + p + 1))
                        for j in range(2):
                            k = 2 * p + j
                            n = gr.g * 32 + 2 * k
                            bank = b_sum[p % 2]
                            aw, ewn = acc[:, bass.ds(starts[k], P)], eacc[:, bass.ds(starts[k], P)]
                            if some(n):
                                dve.wait_ge(added.sem, added.at(q, n))
                            v.tensor_tensor(aw, aw, bank[:, j * P:(j + 1) * P], ALU.add).then_inc(added.sem, 1)
                            v.tensor_tensor(ewn, ewn, bank[0:ED, (2 + j) * P:(3 + j) * P], ALU.add).then_inc(added.sem, 1)

                    for p in range(8):
                        if some(gr.g * 8 + p - 1):
                            dve.wait_ge(agg_mm.sem, agg_mm.at(q, gr.g * 8 + p - 1))
                        for j in range(2):
                            k = 2 * p + j
                            one_hot(gr, k, oh[:, gr.par * GT + k, :], ew).then_inc(oh_made.sem, 1)
                            one_hot(gr, k, ohT[:, p % 2, j * P:(j + 1) * P]).then_inc(oh_made.sem, 1)
                        if p > 0:
                            accumulate(p - 1)
                    accumulate(7)

                each_group(dve, body)
                dve.wait_ge(added.sem, added.at(q, 32 * GROUPS))

            def node_domain(q):
                def attributes(c):
                    mb = (psum[3] if c % 2 == 0 else psum[7])[0:ED, 0:CH]
                    dve.wait_ge(fin_deg.sem, fin_deg.at(q, c + 1))
                    link(v.tensor_scalar(temp(c % 2, 1)[0:ED, :], mb, 1.0, None, ALU.max))
                    link(v.reciprocal(temp(c % 2, 1)[0:ED, :], temp(c % 2, 1)[0:ED, :]))
                    v.tensor_tensor(eacc[:, chunk(c)], eacc[:, chunk(c)], temp(c % 2, 1)[0:ED, :],
                                    ALU.mult).then_inc(fin_attr.sem, 1)

                def maximum(c):
                    par = c % 2
                    mb = (psum[3] if par == 0 else psum[7])[:, 0:CH]
                    dve.wait_ge(fin_loop.sem, fin_loop.at(q, c + 1))
                    if q != GATV2:
                        link(v.scalar_tensor_tensor(out=temp(par, 0), in0=temp(par, 0), scalar=NEG,
                                                    in1=temp(par, 0), op0=ALU.mult, op1=ALU.max))
                    link(v.tensor_tensor(temp(par, 1), mb, temp(par, 0), ALU.max))
                    link(v.tensor_tensor(temp(par, 2), mb, temp(par, 1), ALU.subtract))
                    v.tensor_tensor(temp(par, 3), temp(par, 0), temp(par, 1), ALU.subtract).then_inc(fin_diff.sem, 1)

                def combine(c):
                    par = c % 2
                    hb, _, zb, _ = (b[:, 0:CH] for b in (psum[0:4] if par == 0 else psum[4:8]))
                    ea, eb = temp(par, 4), temp(par, 5)
                    dve.wait_ge(fin_exp.sem, fin_exp.at(q, c + 1))
                    link(v.tensor_tensor(temp(par, 1), zb, ea, ALU.mult))
                    link(v.scalar_tensor_tensor(out=temp(par, 1), in0=temp(par, 1), scalar=1e-16, in1=eb,
                                                op0=ALU.add, op1=ALU.add))
                    link(v.reciprocal(temp(par, 1), temp(par, 1)))
                    if q == GATV2:
                        link(v.scalar_tensor_tensor(out=eb, in0=hb, scalar=vec[:, V_BL:V_BL + 1], in1=eb,
                                                    op0=ALU.add, op1=ALU.mult))
                    else:
                        link(v.tensor_tensor(eb, hb, eb, ALU.mult))
                    link(v.tensor_tensor(ea, acc[:, chunk(c)], ea, ALU.mult))
                    link(v.tensor_tensor(ea, ea, eb, ALU.add))
                    if some(c - 1):
                        dve.wait_ge(fin_out.sem, fin_out.at(q, c - 1))
                    v.tensor_tensor(temp(par, 6), ea, temp(par, 1), ALU.mult).then_inc(fin_sum.sem, 1)

                for c in range(NCH + 1):
                    if c < NCH:
                        if q == GATV2:
                            attributes(c)
                        maximum(c)
                    if c > 0:
                        combine(c - 1)
                dve.wait_ge(fin_out.sem, fin_out.at(q, NCH))

            def divide(q):
                for c in range(NCH):
                    zb = (psum[2] if c % 2 == 0 else psum[6])[:, 0:CH]
                    r = temp(c % 2, 0)
                    dve.wait_ge(fin_mm.sem, fin_mm.at(q, c + 1))
                    link(v.tensor_scalar(r, zb, 1e-30, None, ALU.max))
                    link(v.reciprocal(r, r))
                    v.tensor_tensor(acc[:, chunk(c)], acc[:, chunk(c)], r, ALU.mult).then_inc(fin_sum.sem, 1)

            def graph_norm(q):
                link(v.tensor_reduce(gn[:, 0:1], acc[:, 0:NODES], AX_X, ALU.add))
                link(v.tensor_scalar(gn[:, 1:2], gn[:, 0:1], -1.0 / NODES, None, ALU.mult))
                v.tensor_tensor(gn[:, 2:3], gn[:, 1:2], vec[:, V_GM:V_GM + 1], ALU.mult).then_inc(gn_mean.sem, 1)
                dve.wait_ge(gn_sq.sem, gn_sq.at(q, 1))
                v.tensor_scalar(gn[:, 4:5], gn[:, 3:4], 1.0 / NODES, EPS, ALU.mult, ALU.add).then_inc(gn_var.sem, 1)
                dve.wait_ge(gn_std.sem, gn_std.at(q, 1))
                link(v.reciprocal(gn[:, 5:6], gn[:, 5:6]))
                link(v.tensor_tensor(gn[:, 6:7], gn[:, 5:6], vec[:, V_GW:V_GW + 1], ALU.mult))
                v.scalar_tensor_tensor(out=gn[:, 7:8], in0=gn[:, 6:7], scalar=gn[:, 2:3],
                                       in1=vec[:, V_GB:V_GB + 1], op0=ALU.mult, op1=ALU.add).then_inc(
                    gn_scale.sem, 1)

            def residual(q):
                for b in range(NB):
                    n = len(batch(b))
                    i0 = TB * b
                    bank = (b_oht, b_feat)[b % 2]
                    got = bank[0:NP, 0:n * D].rearrange("p (i f) -> p i f", f=D)
                    xs = x[0:NP, i0:i0 + n, :]
                    dve.wait_ge(res_turned.sem, res_turned.at(q, b + 1))
                    if q == GCN:
                        for j in range(n):
                            link(v.scalar_tensor_tensor(out=temp(0, j)[0:NP, 0:D], in0=got[:, j, :],
                                                        scalar=norm[0:NP, 1, i0 + j:i0 + j + 1],
                                                        in1=brow[0:NP, R_G:R_G + D], op0=ALU.mult, op1=ALU.add))
                            last = v.scalar_tensor_tensor(out=x[0:NP, i0 + j, :], in0=temp(0, j)[0:NP, 0:D],
                                                          scalar=0.0, in1=x[0:NP, i0 + j, :], op0=ALU.max,
                                                          op1=ALU.add)
                    elif q == ATTN:
                        if some(b - 1):
                            dve.wait_ge(res_added.sem, res_added.at(q, b - 1))
                        t = temp(b % 2, 0, 2)[0:NP, 0:n * D].rearrange("p (i f) -> p i f", f=D)
                        link(v.tensor_tensor(t, got, brow[0:NP, R_O:R_O + D].unsqueeze(1).to_broadcast([NP, n, D]),
                                             ALU.add))
                        last = v.tensor_tensor(xs, xs, t, ALU.add)
                    else:
                        last = v.tensor_tensor(xs, xs, got, ALU.add)
                    last.then_inc(res_added.sem, 1)
                dve.wait_ge(res_added.sem, res_added.at(q, NB))

            def degrees(q):
                dve.wait_ge(deg_turned.sem, deg_turned.at(q, 1))
                v.tensor_scalar(norm[0:NP, 0, :], b_w[0:NP, 0:9 * NI].rearrange("p (i z) -> p i z", z=9)[:, :, 8],
                                1.0, None, ALU.max).then_inc(deg_made.sem, 1)
                dve.wait_ge(deg_root.sem, deg_root.at(q, 1))
                v.reciprocal(norm[0:NP, 1, :], norm[0:NP, 1, :]).then_inc(deg_made.sem, 1)
                dve.wait_ge(deg_made.sem, deg_made.at(q, 2))

            statistics(GAT1)
            hidden(GAT1)
            clear(GAT1)
            softmax_pass(GAT1)
            node_domain(GAT1)
            clear(GAT2)
            softmax_pass(GAT2)
            node_domain(GAT2)
            residual(GAT2)
            degrees(GCN)
            statistics(GCN)
            hidden(GCN)
            clear(GCN)
            gcn_pass(GCN)
            residual(GCN)
            statistics(GATV2)
            hidden(GATV2)
            table(GATV2)
            clear(GATV2)
            softmax_pass(GATV2)
            node_domain(GATV2)
            graph_norm(GATV2)
            residual(GATV2)
            statistics(ATTN)
            hidden(ATTN)
            table(ATTN)
            clear(ATTN)
            softmax_pass(ATTN)
            divide(ATTN)
            residual(ATTN)


def kernel(**inputs):
    import numpy as np
    import concourse.bacc as bacc
    from concourse.bass_utils import run_bass_kernel_spmd as run

    arr = {k: np.ascontiguousarray(a) for k, a in inputs.items()}
    pad = EPAD - EDGES
    dst = np.concatenate([arr["dst"], np.full(pad, NODES, np.int32)])
    src = np.concatenate([arr["src"], np.zeros(pad, np.int32)])
    attr = np.concatenate([arr["edge_attr_64"], np.zeros((pad, ED), np.float32)])
    ew = np.concatenate([arr["edge_weight1"][:, 0], np.zeros(pad, np.float32)])
    edge_of = np.array([-1], np.int32)
    f = np.arange(P)
    cst = np.zeros((P, C_END), np.float32)
    cst[:, C_ID:C_ID + P] = np.eye(P)
    cst[:, C_IOTA:C_IOTA + P] = f[None, :]
    cst[:, C_SAME:C_SAME + P] = f[:, None] // 32 == f[None, :] // 32
    cst[:, C_HM4:C_HM4 + 4] = f[:, None] // 32 == f[None, 0:4]
    cst[:, C_HM8:C_HM8 + 8] = f[:, None] % 8 == f[None, 0:8]
    cst[:, C_TM:C_TM + GT] = f[:, None] % GT == f[None, 0:GT]
    cst[:, C_HX4:C_HX4 + P] = f[:, None] // GT == f[None, :] // 32
    cst[:, C_HX8:C_HX8 + P] = f[:, None] // GT == f[None, :] % 8
    cst[:, C_HZ:C_HZ + 8] = f[:, None] // GT == f[None, 0:8]
    cst[0:4, C_SZ4:C_SZ4 + P] = f[0:4, None] == f[None, :] // 32
    cst[4:8, C_SM4:C_SM4 + P] = f[0:4, None] == f[None, :] // 32
    cst[8, C_SD:C_SD + P] = 1
    cst[0:8, C_SZ8:C_SZ8 + P] = f[0:8, None] == f[None, :] % 8
    cst[:, C_ONE] = 1
    w = np.concatenate([
        arr["L0_gnn_W1"], arr["L0_gnn_W1"].T, arr["L0_gnn_W2"], arr["L0_gnn_W2"].T, arr["L1_gnn_W"],
        arr["L2_gnn_Wl"], arr["L2_gnn_Wr"], arr["L3_gnn_Wk"].T, arr["L3_gnn_Wv"].T, arr["L3_gnn_Wq"].T,
        arr["L3_gnn_Wo"].T], axis=1)
    vec = np.stack([arr[n].reshape(-1) for n in (
        "L0_gnn_a_src1", "L0_gnn_a_dst1", "L0_gnn_b1", "L0_gnn_a_src2", "L0_gnn_a_dst2", "L0_gnn_b2",
        "L2_gnn_bl", "L2_gnn_br", "L2_gnn_att", "L2_gnn_bias_out", "L2_gnn_gn_weight", "L2_gnn_gn_bias",
        "L2_gnn_gn_mean_scale")], axis=1)
    rows = np.concatenate([arr[n] for n in (
        "L1_gnn_b", "L2_gnn_bl", "L2_gnn_br", "L3_gnn_bk", "L3_gnn_bv", "L3_gnn_bq", "L3_gnn_bo")])[None, :]
    data = {
        "x": arr["x"],
        "src_idx": src.reshape(TILES, P).T,
        "dst_tile": dst.reshape(TILES, P).T,
        "dst_first": dst[::P][None, :],
        "dst_last": dst[P - 1::P][None, :],
        "dst_last_prev": np.concatenate([edge_of, dst[P - 1:-1:P]])[None, :],
        "dst_flat": np.concatenate([edge_of, dst, edge_of]),
        "edge_attr": attr.reshape(TILES, P, ED).transpose(1, 0, 2).reshape(P, TILES * ED),
        "edge_attr_t": attr.T,
        "edge_weight": ew.reshape(TILES, P).T,
        "weights": w, "w_edge": arr["L2_gnn_We"], "vectors": vec, "bias_rows": rows, "consts": cst,
    }
    nc = bacc.Bacc("TRN2", target_bir_lowering=False, num_devices=1)
    arrays, args = {}, []
    for name, a in data.items():
        a = np.ascontiguousarray(a)
        arrays[f"in_{name}_dram"] = a
        args.append(nc.dram_tensor(f"in_{name}_dram", a.shape, mybir.dt.from_np(a.dtype), kind="ExternalInput").ap())
    args.append(nc.dram_tensor("out_0_dram", (NODES, D), F32, kind="ExternalOutput").ap())
    build(nc, *args)
    r = run(nc, [arrays], core_ids=[0])
    return r.results[0]["out_0_dram"]
```

```python
from contextlib import ExitStack

import concourse.bass as bass
from concourse import mybir

ALU = mybir.AluOpType
ACT = mybir.ActivationFunctionType
AX_X = mybir.AxisListType.X
F32 = mybir.dt.float32
I32 = mybir.dt.int32
BF16 = mybir.dt.bfloat16

P = 128
NODES = 3125
EDGES = 53125
D = 128
ED = 64
NP = 125
NI = NODES // NP
GT = 16
TILES = -(-EDGES // (P * GT)) * GT
GROUPS = TILES // GT
QT = 4
EPAD = TILES * P
TROWS = NODES + P
CH = 448
NCH = 7
NCOL = NCH * CH
ACOL = GROUPS * P
BIG = 1e38
NEG = 0.2
EPS = 1e-5
TB = 4
NB = -(-NI // TB)
TC = 5
TS = 4
VROW = 256
assert NP * NI == NODES and TILES == ACOL // P * GT and GROUPS % 2 == 0 and NCOL + P <= ACOL

GAT1, GAT2, GCN, GATV2, ATTN = range(5)
SOFTMAX = (GAT1, GAT2, GATV2, ATTN)
LN_OF = {GAT1: 0, GCN: 1, GATV2: 2, ATTN: 3}
HEADS = {GAT1: 4, GAT2: 4, GATV2: 4, ATTN: 8}
TF = {GAT1: 136, GAT2: 136, GCN: 128, GATV2: 256, ATTN: 384}
ZR = 27
WP = 12
ROWF = {GAT1: 132, GAT2: 132, GCN: 128, GATV2: 128, ATTN: 256}
WINF = {GAT1: WP, GAT2: WP, GATV2: 128, ATTN: 128}
VOFF = {GAT1: 0, GAT2: 0, GCN: 0, GATV2: 0, ATTN: 128}

C_ID, C_IOTA, C_SAME, C_HM4, C_HM8, C_HX4, C_HX8, C_HZ, C_SZ4, C_SM4, C_SD, C_SZ8, C_DB, C_END = (
    0, 128, 256, 384, 388, 396, 524, 652, 679, 807, 935, 1063, 1191, 1192)
(V_AS1, V_AD1, V_B1, V_AS2, V_AD2, V_B2, V_BL, V_BR, V_ATT, V_BO, V_GW, V_GB, V_GM) = range(13)
(W_1, W_1T, W_2, W_2T, W_G, W_L, W_R, W_K, W_V, W_Q, W_O) = range(11)
W_LR = W_1T
STEPS = {GATV2: {"add": (1, 3, 7, 11), "leaky": (2, 5, 9, 13), "times": (4, 8, 12, 15), "sum": (6, 10, 14, 16)},
         ATTN: {"times": (1, 2, 4, 6), "sum": (3, 5, 7, 8)}}
NSTEP = {GATV2: 16, ATTN: 8}
R_G, R_LR, R_KVQ, R_O, R_ATT, R_END = 0, 128, 384, 768, 896, 1024


class Signal:

    def __init__(self, sem, totals):
        self.sem, self.totals = sem, totals

    def at(self, phase, n):
        return sum(self.totals.get(q, 0) for q in range(phase)) + n


def some(n):
    return not isinstance(n, int) or n > 0


class Group:

    def __init__(self, g, par, half):
        self.g, self.par, self.half = g, par, half


class Path:

    def __init__(self, tiles, nodes, added, softmax_adds, gcn_adds):
        self.tiles, self.nodes, self.added = tiles, nodes, added
        self.softmax_adds, self.gcn_adds = softmax_adds, gcn_adds


def each_group(eng, body, tail=None):
    zero, one = Group(0, 0, 0), Group(1, 1, 0)
    body(zero, None)
    body(one, zero)
    with eng.Fori(1, GROUPS // 2) as it:
        even, odd = Group(it * 2, 0, it), Group(it * 2 + 1, 1, it)
        body(even, Group(it * 2 - 1, 1, it - 1))
        body(odd, even)
    if tail is not None:
        tail(Group(GROUPS - 1, 1, GROUPS // 2 - 1))


def build(nc, x_in, src_idx, dst_tile, dst_first, quarter_first, quarter_last, dst_last, dst_last_prev, dst_flat, edge_attr, edge_attr_t,
          edge_weight, weights, w_edge, vectors, bias_rows, consts, out):
    with ExitStack() as ctx:
        def sb(name, shape, dt=F32):
            return ctx.enter_context(nc.sbuf_tensor(name, shape, dt))

        def sem(name):
            return ctx.enter_context(nc.semaphore(name))

        def dram(name, shape):
            return nc.dram_tensor(name, shape, F32, kind="Internal").ap()

        gtab = {p: dram(f"gather_table{p}", (NODES, ROWF[p])) for p in ROWF}
        wtab = {p: nc.dram_tensor(f"window_table{p}", (TROWS, WINF[p]), BF16 if p in (GAT1, GAT2) else F32,
                                  kind="Internal").ap() for p in WINF}

        x = sb("x", [P, NI, D])
        hT = sb("hT", [P, NCOL])
        acc = sb("acc", [P, ACOL])
        zacc_mem = sb("zacc", [P, ACOL])
        eacc_mem = sb("eacc", [P, ACOL])
        vring = sb("gathered_rows", [P, 2 * GT, VROW])
        oh_mem = sb("one_hot", [P, 3 * GT // 2 * P])
        ohT = sb("one_hot_t", [P, 2, 4 * P])
        tq_sb = sb("edge_features", [P, 2, 4 * P])
        win = sb("window_rows", [P, 8, D])
        ering = sb("edge_attr_ring", [P, 2, GT * ED])
        msg = sb("messages", [P, 2, QT, D])
        wm = sb("weights_and_max", [P, 2, GT, ZR], BF16)
        wrest = sb("weights_rest", [P, P])
        wsplit = sb("window_parts", [NP, TS, TC, WP], BF16)
        wsrest = sb("window_rest", [NP, TS, TC, 4])
        iota_b = sb("iota", [P, P], BF16)
        ident_b = sb("identity", [P, P], BF16)
        s_sb = sb("scores", [P, P])
        s_tmp = sb("scores_sum", [P, P])
        fwd = sb("running_max", [P, P])
        bwd = sb("tile_max", [P, P])
        shift = sb("shift", [P, P])
        diff = sb("diff", [P, P + 1])
        wexp = sb("chunk_weights", [P, P + 1])
        mend = sb("end_max", [P, P])
        resc = sb("rescale", [P, 2, 2])
        start_pen = sb("start_pen", [P, ACOL], BF16)
        end_pen = sb("end_pen_reversed", [P, ACOL], BF16)
        first_pen = sb("first_pen", [P, ACOL], BF16)
        last_pen = sb("last_pen", [P, ACOL], BF16)
        is_end = sb("is_end", [P, ACOL], BF16)
        cin = sb("carry_in", [1, 8, GT + 1])
        crow = sb("carry_row", [1, 8, GT + 1])
        cshift = sb("carry_shifted", [1, 8 * GT])
        first_row = sb("first_row", [1, 8 * GT])
        rrow = sb("first_max", [1, 8 * GT])
        rnext = sb("next_first_max", [1, 8 * GT])
        row_pen = sb("row_pen", [1, GROUPS, GT + 1], BF16)
        back_pen = sb("back_pen_reversed", [1, GROUPS, GT], BF16)
        row_pen_h = sb("row_pen_by_head", [1, 8 * (GT + 1)])
        back_pen_h = sb("back_pen_by_head", [1, 8 * GT])
        cont_pen = sb("cont_pen", [1, TILES])
        idx_all = sb("src_index", [P, TILES], I32)
        idx = sb("src_index_ring", [P, 2, GT], I32)
        dfirst = sb("dst_first", [1, TILES], I32)
        qfirst = sb("quarter_first", [1, TILES // QT], I32)
        span = sb("quarter_span", [1, TILES // QT], I32)
        narrow = sb("all_narrow", [1, 1], I32)
        drel = sb("dst_relative", [P, TILES], BF16)
        ew = sb("edge_weight", [P, TILES])
        cst = sb("constants", [P, C_END])
        wts = sb("weights", [P, 11, D])
        we = sb("w_edge", [ED, D])
        vec = sb("vectors", [P, 13])
        brow = sb("bias_rows", [P, R_END])
        gat_cols = sb("gat_cols", [P, 2, 8])
        gat_rep = sb("gat_same_head", [P, 2, D])
        gat_w = sb("gat_w", [P, 2, 136])
        gat_wrep = sb("gat_w_loop", [P, 2, D])
        att_rep = sb("att_same_head", [P, D])
        blr = sb("bl_plus_br", [P, 1])
        stat = sb("ln_stat", [P, NI, 6])
        mv = sb("ln_mean_var", [P, NI, 2])
        lnv = sb("ln_vectors", [P, 4, NI])
        norm = sb("norm", [P, 2, NI])
        gn = sb("graph_norm", [P, 8])

        hn = oh_mem[0:NP, 0:8 * P].rearrange("p (a b) -> p a b", b=P)
        oh_flat = oh_mem[:, :].bitcast(I32)
        oh = oh_mem[:, 0:GT * P].bitcast(BF16).rearrange("p (a b) -> p a b", b=P)
        oh_wide = oh_mem[:, GT * P:3 * GT // 2 * P].rearrange("p (s e) -> p s e", s=2)
        oh_gcn = oh_mem[:, 0:2 * QT * P].rearrange("p (s e) -> p s e", s=2)
        ohT_b = ohT[:, 0, :].bitcast(BF16).rearrange("p (s e) -> p s e", s=2)
        win_b = win[:, :, :].rearrange("p a b -> p (a b)").bitcast(BF16)[:, 0:2 * GT * WP].rearrange(
            "p (s f) -> p s f", f=WP)
        dtile, dfirst_b = oh_flat[:, 8 * P:8 * P + TILES], oh_flat[:, 8 * P + TILES:8 * P + 2 * TILES]
        last_i = oh_flat[0:1, 8 * P + 2 * TILES:8 * P + 4 * TILES].rearrange("p (s t) -> p s t", s=2)
        kt_sb = ering[:, :, 4 * P:8 * P]
        tab = vring[0:NP, :, :].rearrange("p a b -> p (a b)")[:, 0:TS * TC * 384].rearrange(
            "p (s i f) -> p s i f", s=TS, i=TC)
        vflat = vring[:, :, :].rearrange("p a b -> p (a b)")

        zacc, eacc = zacc_mem[0:ZR, :], eacc_mem[0:ED, :]

        d_cur = acc[:, :].bitcast(I32).rearrange("p (g e) -> p g e", e=P)
        d_prev = eacc_mem[:, :].bitcast(I32).rearrange("p (g e) -> p g e", e=P)
        d_next = zacc_mem[:, :].bitcast(I32).rearrange("p (g e) -> p g e", e=P)

        def temp(par, n, w=1):
            at = (par * 8 + n) * CH
            return vflat[:, at:at + w * CH]

        ident = cst[:, C_ID:C_ID + P]
        tq_flat = tq_sb[:, :, :].rearrange("p s e -> p (s e)")
        end_pen_r = end_pen[:, :].rearrange("p (g e) -> p g e", e=P)[:, :, ::-1]
        psum = [ctx.enter_context(nc.psum_tensor(f"bank{b}", [P, 512], F32)) for b in range(8)]
        b_oht, b_feat, b_keys, b_small, b_sum0, b_sum1, b_e, b_w = psum
        b_sum = (b_sum0, b_sum1)
        b_table = (b_keys, b_e, b_sum0, b_sum1)
        p_score, p_chunk = b_small[:, 0:128], b_small[:, 128:256]
        p_last, p_first = b_small[0:1, 256:384], b_small[0:1, 384:512]
        p_carry, p_own, p_next = (b_small[:, n:n + 1] for n in range(3))
        p_resc, p_rescz = b_small[:, 8:9], b_small[0:ZR, 9:10]
        p_feat = (b_feat, b_keys)
        p_oht = [[b[:, :].bitcast(BF16)[:, 0:4 * P] for b in (b_oht, b_keys if q in (GAT1, GAT2) else b_oht)] for q in range(5)]
        p_wm = (b_e[:, 0:128], b_w[:, 0:128])

        ALL = range(5)
        per_group = lambda n, phases=SOFTMAX: {q: n * GROUPS for q in phases}

        def signal(name, totals):
            return Signal(sem(name), totals)

        def turned(path, q, t):
            if path is NARROW and q == GATV2:
                return ohT[:, t, :] if t < 2 else ering[:, t - 2, 0:4 * P]
            return ohT[:, t % 2, :]

        def turned_before(path, q, t):
            return t - 3 if path is NARROW and q == GATV2 else t - 1

        NARROW = Path(QT, 48, signal("accumulated_narrow", {**per_group(10), GCN: 8 * GROUPS}), 10, 8)
        WIDE = Path(1, P, signal("accumulated_wide", {**per_group(34), GCN: 32 * GROUPS}), 34, 32)

        first_loaded = sem("first_inputs_loaded")
        loaded = sem("inputs_loaded")
        setup = sem("dve_setup")
        narrow_known = sem("narrow_known")
        drel_made = sem("dst_relative_made")
        waited = sem("waited_apart")
        link_sem = sem("dve_chain")
        prepared = sem("weights_prepared")
        gat_mm = sem("gat_weight_products")
        zeroed = sem("window_pads_stored")
        ln_stats = signal("ln_statistics", {q: 1 for q in LN_OF})
        ln_var = signal("ln_variance", {q: 1 for q in LN_OF})
        ln_std = signal("ln_deviation", {q: 1 for q in LN_OF})
        hn_made = signal("normalized", {q: NI for q in LN_OF})
        hn_turned = signal("normalized_transposed", {q: NB for q in LN_OF})
        ht_made = signal("hT_written", {q: NB for q in LN_OF})
        tab_mm = signal("table_product", {q: NI for q in ALL})
        tab_made = signal("table_rows", {q: NI for q in ALL})
        win_split = signal("window_parts_made", {GAT1: TC, GAT2: TC})
        tab_stored = [sem(f"table_stored{s}") for s in range(TS)]
        deg_turned = signal("degree_transposed", {GCN: 1})
        deg_made = signal("degree", {GCN: 2})
        deg_root = signal("degree_root", {GCN: 1})
        idx_copied = signal("src_index_copied", {q: GROUPS for q in ALL})
        rows_in = [[signal(f"rows_gathered{a}{b}", {q: 64 * GROUPS // 2 for q in ALL}) for b in range(4)]
                   for a in range(2)]
        win_in = [signal(f"window_loaded{k}", per_group(16)) for k in range(GT)]
        ea_in = [signal(f"edge_attr_loaded{s}", {GCN: 16 * GROUPS // 2 if s < 2 else 0, GATV2: 16 * GROUPS}) for s in range(4)]
        oh_made = signal("one_hot_made", {**per_group(4), GCN: 8 * GROUPS})
        oh_turned = signal("one_hot_transposed", per_group(4))
        oh_copied = signal("one_hot_t_copied", per_group(4))
        feat_mm = signal("edge_features_product", per_group(4))
        score_step = signal("score_steps", {q: NSTEP[q] * GROUPS for q in NSTEP})
        we_in = sem("w_edge_in_windows")
        gap_zero = sem("rows_below_one_hots_zero")
        score_sum = signal("score_summed", per_group(1, (GAT1, GAT2)))
        score_out = signal("scores_copied", per_group(1, (GAT1, GAT2)))
        chunk_in = signal("scores_transposed", per_group(1))
        fwd_made = signal("running_max_made", per_group(1))
        bwd_made = signal("tile_max_made", per_group(1))
        last_turned = signal("last_max_transposed", per_group(1))
        last_copied = signal("last_max_copied", per_group(1))
        carry_made = signal("carry_made", per_group(1))
        carry_out = signal("carry_shifted_made", per_group(3))
        carry_turned = signal("carry_transposed", per_group(1))
        shift_part = signal("shift_without_next", per_group(1))
        shift_made = signal("shift_made", per_group(1))
        diff_made = signal("diff_made", per_group(2))
        mend_made = signal("end_max_made", per_group(1, (GAT1, GAT2, GATV2)))
        wexp_made = signal("chunk_weights_made", per_group(1))
        w_turned = signal("weights_transposed", per_group(1))
        oh_widened = signal("one_hot_widened", per_group(4))
        wm_hi = signal("weights_high_part", per_group(1))
        wm_rest = signal("weights_rest_made", per_group(1))
        wm_mid = signal("weights_middle_part", per_group(1))
        wm_low = signal("weights_low_part", per_group(1))
        pens_made = signal("row_pens_by_head_made", per_group(2))
        row_made = signal("first_row_made", per_group(1))
        own_made = signal("first_max_made", per_group(1))
        resc_mm = signal("rescale_product", per_group(1))
        resc_copied = signal("rescale_copied", per_group(2))
        msg_made = signal("messages_made", per_group(4))
        agg_mm = signal("aggregate_product", {q: 4 * GROUPS for q in ALL})
        cleared = signal("accumulators_cleared", {GAT1: 3, GAT2: 3, GCN: 2, GATV2: 3, ATTN: 3})
        fin_deg = signal("loop_degree_product", {GATV2: NCH})
        fin_attr = signal("loop_attr_made", {GATV2: NCH})
        fin_feat = signal("loop_features_product", {GATV2: NCH})
        fin_biased = signal("loop_features_biased", {GATV2: NCH})
        fin_leaky = signal("loop_features_leaky", {GATV2: NCH})
        fin_mm = signal("node_products", {GAT1: NCH, GAT2: NCH, GATV2: NCH, ATTN: NCH})
        fin_parts = signal("node_diff_parts", {GAT1: NCH, GAT2: NCH, GATV2: NCH})
        fin_diff = signal("node_diff", {GAT1: NCH, GAT2: NCH, GATV2: NCH})
        fin_exp = signal("node_exp", {GAT1: NCH, GAT2: NCH, GATV2: NCH})
        fin_sum = signal("node_sum", {GAT1: NCH, GAT2: NCH, GATV2: NCH, ATTN: NCH})
        fin_out = signal("node_out", {GAT1: NCH, GAT2: NCH, GATV2: NCH})
        gn_mean = signal("graph_mean", {GATV2: 1})
        gn_sq = signal("graph_square_sum", {GATV2: 1})
        gn_var = signal("graph_variance", {GATV2: 1})
        gn_std = signal("graph_deviation", {GATV2: 1})
        gn_scale = signal("graph_scale", {GATV2: 1})
        gn_out = signal("graph_norm_out", {GATV2: 1})
        res_turned = signal("residual_transposed", {GAT2: NB, GCN: NB, GATV2: NB, ATTN: NB})
        res_added = signal("residual_added", {GAT2: NB, GCN: NB, GATV2: NB, ATTN: NB})
        out_stored = sem("out_stored")

        FIRST, LOADS = 8, 7 + 3 * 8
        def tab_count(phase, chunk, slot):
            n = 0
            for q in range(phase + 1):
                for c in range(TC if q < phase else chunk + 1):
                    if c % TS == slot:
                        n += 16 * (2 if q in WINF else 1)
            return n

        def slot_count(phase, c):
            if c >= TS:
                return tab_count(phase, c - TS, c % TS)
            return tab_count(phase - 1, TC - 1, c % TS) if phase > 0 else 0

        def sums_of(path, u, j, rows):
            if path is NARROW:
                bank = b_sum[u % 2]
                return bank[:, 0:path.nodes], bank[0:rows, path.nodes:2 * path.nodes]
            return b_sum0[:, j * P:(j + 1) * P], b_sum1[0:rows, j * P:(j + 1) * P]

        def sums_free(path, u, g, adds):
            first = adds - (8 if path is NARROW else 32)
            if path is NARROW:
                return g * adds + (first + 2 * (u - 1) if u > 1 else 2 * u - 2)
            return g * adds + (first + 8 * u if u > 0 else 0)

        def batch(b):
            return range(TB * b, min(TB * b + TB, NI))

        def chunk(c):
            return slice(c * CH, (c + 1) * CH)

        block = ctx.enter_context(nc.Block())

        @block.sync
        def _(sp):
            regs = [sp.alloc_register(f"window{k}") for k in range(GT)]
            sp.dma_start(qfirst[:, :], quarter_first[:, :]).then_inc(first_loaded, 16)
            sp.dma_start(span[:, :], quarter_last[:, :]).then_inc(first_loaded, 16)
            sp.dma_start(x[0:NP, :, :], x_in.rearrange("(p i) f -> p i f", i=NI)).then_inc(first_loaded, 16)
            sp.dma_start(vec[:, :], vectors[:, :]).then_inc(first_loaded, 16)
            sp.dma_start(cst[:, :], consts[:, :]).then_inc(first_loaded, 16)
            sp.dma_start(wts[:, :, :], weights.rearrange("p (n f) -> p n f", n=11)).then_inc(first_loaded, 16)
            sp.dma_start(we[:, :], w_edge[:, :]).then_inc(first_loaded, 16)
            sp.dma_start(brow[:, :], bias_rows[0:1, :].to_broadcast([P, R_END])).then_inc(first_loaded, 16)
            sp.dma_start(idx_all[:, :], src_idx[:, :]).then_inc(loaded, 16)
            sp.dma_start(dtile[:, :], dst_tile[:, :]).then_inc(loaded, 16)
            sp.dma_start(dfirst_b[:, :], dst_first[0:1, :].to_broadcast([P, TILES])).then_inc(loaded, 16)
            sp.dma_start(dfirst[:, :], dst_first[:, :]).then_inc(loaded, 16)
            sp.dma_start(last_i[:, 0, :], dst_last[:, :]).then_inc(loaded, 16)
            sp.dma_start(last_i[:, 1, :], dst_last_prev[:, :]).then_inc(loaded, 16)
            sp.dma_start(ew[:, :], edge_weight[:, :]).then_inc(loaded, 16)
            for d, off in ((d_cur, 1), (d_prev, 0), (d_next, 2)):
                by_chunk = dst_flat[off:off + EPAD].rearrange("(g t e) -> t g e", t=GT, e=P)
                for h in range(8):
                    sp.dma_start(d[GT * h:GT * (h + 1), :, :], by_chunk).then_inc(loaded, 16)
            sp.wait_ge(setup, 1)
            for q in WINF:
                pads = s_tmp[:, 0:WINF[q]] if q in (GATV2, ATTN) else s_tmp[:, 0:WP // 2].bitcast(BF16)
                sp.dma_start(wtab[q][NODES:TROWS, :], pads).then_inc(zeroed, 16)
            sp.wait_ge(zeroed, 16 * len(WINF))
            sp.wait_ge(loaded, 16 * LOADS)

            def layers(path):
                W, added = path.nodes, path.added

                def store_tables(q):
                    for c in range(TC):
                        s = c % TS
                        sp.wait_ge(tab_made.sem, tab_made.at(q, TC * (c + 1)))
                        g = gtab[q][0:NODES, :].rearrange("(p i) f -> p i f", i=NI)[:, TC * c:TC * (c + 1), :]
                        sp.dma_start(g, tab[:, s, :, 0:ROWF[q]]).then_inc(tab_stored[s], 16)
                        if q in WINF:
                            w = wtab[q][0:NODES, :].rearrange("(p i) f -> p i f", i=NI)[:, TC * c:TC * (c + 1), :]
                            if q in (GAT1, GAT2):
                                sp.wait_ge(win_split.sem, win_split.at(q, c + 1))
                                sp.dma_start(w, wsplit[:, s, :, :]).then_inc(tab_stored[s], 16)
                            else:
                                sp.dma_start(w, tab[:, s, :, ROWF[q]:TF[q]]).then_inc(tab_stored[s], 16)

                def windows(gr):
                    n = GT // path.tiles
                    firsts = qfirst if path is NARROW else dfirst
                    sp.load(regs[0:n], firsts[0:1, bass.ds(gr.g * n, n)])
                    return [sp.snap(r, min_val=0, max_val=NODES) for r in regs[0:n]]

                def load_w_edge():
                    sp.dma_start(win[ED:, :, :], w_edge.unsqueeze(1).to_broadcast([ED, 8, D])).then_inc(we_in, 16)

                def load_windows(q):
                    for s in range(TS):
                        sp.wait_ge(tab_stored[s], tab_count(q, TC - 1, s))

                    def body(gr, before):
                        starts = windows(gr)
                        if q in (GAT1, GAT2):
                            if some(gr.g * 4 - 4):
                                sp.wait_ge(feat_mm.sem, feat_mm.at(q, gr.g * 4 - 4))
                                sp.sem_inc(waited, 1)
                        for t in range(4):
                            if q in (GATV2, ATTN):
                                if some(gr.g * 4 + turned_before(path, q, t)):
                                    sp.wait_ge(feat_mm.sem, feat_mm.at(q, gr.g * 4 + turned_before(path, q, t)))
                                    sp.sem_inc(waited, 1)
                            if q == GATV2:
                                e0 = gr.g * (GT * P) + t * 4 * P
                                place = turned(path, q, t)[ED:, :] if path is NARROW else ering[0:ED, t % 2, 0:4 * P]
                                sp.dma_start(place, edge_attr_t[:, bass.ds(e0, 4 * P)]).then_inc(
                                    ea_in[t].sem, 16)
                            K = ED if path is NARROW and q == GATV2 else W
                            for n in range(QT // path.tiles * t, QT // path.tiles * (t + 1)):
                                slot = (win_b[:W, gr.par * GT + n, :] if q in (GAT1, GAT2) else
                                        win[:K, gr.par * 4 + n if path is NARROW else n % 8, :])
                                if some(gr.g * 16):
                                    sp.wait_ge(win_in[n].sem, win_in[n].at(q, gr.g * 16))
                                sp.dma_start(slot, wtab[q][bass.ds(starts[n], K), :]).then_inc(win_in[n].sem, 16)

                    each_group(sp, body)

                def load_edge_attr(q):
                    def body(gr, before):
                        if some(gr.g * 4 - 4):
                            sp.wait_ge(agg_mm.sem, agg_mm.at(q, gr.g * 4 - 4))
                        v = edge_attr[:, bass.ds(gr.g * (GT * ED), GT * ED)]
                        sp.dma_start(ering[:, gr.par, :], v).then_inc(ea_in[gr.par].sem, 16)

                    each_group(sp, body)

                for q in ALL:
                    store_tables(q)
                    if q == GATV2 and path is NARROW:
                        load_w_edge()
                    if q in WINF:
                        load_windows(q)
                    else:
                        load_edge_attr(q)
                sp.wait_ge(res_added.sem, res_added.at(ATTN, NB))
                sp.dma_start(out.rearrange("(p i) f -> p i f", i=NI), x[0:NP, :, :]).then_inc(out_stored, 16)
                sp.wait_ge(out_stored, 16)

            sp.wait_ge(narrow_known, 1)
            all_narrow = sp.value_load(narrow[0:1, 0:1], min_val=0, max_val=1)
            with sp.If(all_narrow > 0):
                layers(NARROW)
            with sp.Else():
                layers(WIDE)

        @block.gpsimd
        def _(pool):
            pool.wait_ge(loaded, 16 * LOADS)
            def layers(path):
                W, added = path.nodes, path.added

                for q in ALL:
                    for s in range(TS):
                        pool.wait_ge(tab_stored[s], tab_count(q, TC - 1, s))

                    def body(gr, before):
                        for b in range(4):
                            if some(gr.half * 64):
                                pool.wait_ge(rows_in[gr.par][b].sem, rows_in[gr.par][b].at(q, gr.half * 64))
                        if some(gr.g):
                            pool.wait_ge(idx_copied.sem, idx_copied.at(q, gr.g))
                        nc.gpsimd.tensor_copy(idx[:, gr.par, :], idx_all[:, bass.ds(gr.g * GT, GT)]).then_inc(
                            idx_copied.sem, 1)
                        pool.wait_ge(idx_copied.sem, idx_copied.at(q, gr.g + 1))
                        for k in range(GT):
                            if k % QT == 0:
                                used = agg_mm if q == GCN else msg_made
                                if some(gr.g * 4 - 8 + k // QT + 1):
                                    pool.wait_ge(used.sem, used.at(q, gr.g * 4 - 8 + k // QT + 1))
                                    pool.sem_inc(waited, 1)
                            pool.indirect_dma_start(
                                vring[:, gr.par * GT + k, 0:ROWF[q]], None, gtab[q][:, :],
                                bass.IndirectOffsetOnAxis(ap=idx[:, gr.par, k:k + 1], axis=0),
                            ).then_inc(rows_in[gr.par][k // 4].sem, 16)

                    each_group(pool, body)

            pool.wait_ge(narrow_known, 1)
            all_narrow = pool.value_load(narrow[0:1, 0:1], min_val=0, max_val=1)
            with pool.If(all_narrow > 0):
                layers(NARROW)
            with pool.Else():
                layers(WIDE)

        @block.tensor
        def _(pe):
            mm, tr = nc.tensor.matmul, nc.tensor.transpose

            def wt(n):
                return wts[:, n, :]

            pe.wait_ge(first_loaded, 16 * FIRST)
            pe.wait_ge(prepared, 1)
            for n, w in ((0, W_1T), (1, W_2T)):
                mm(b_oht[:, 256 * n:256 * n + 8], wt(w), gat_cols[:, n, :], start=True, stop=True)
                mm(b_oht[:, 256 * n + 128:256 * n + 256], wt(w), gat_rep[:, n, :], start=True,
                   stop=True).then_inc(gat_mm, 1)

            def layers(path):
                W, added = path.nodes, path.added

                def turn_hidden(q):
                    for b in range(NB):
                        pe.wait_ge(hn_made.sem, hn_made.at(q, batch(b)[-1] + 1))
                        if some(b - 1):
                            pe.wait_ge(ht_made.sem, ht_made.at(q, b - 1))
                        bank = (b_oht, b_feat)[b % 2]
                        for j, i in enumerate(batch(b)):
                            last = tr(bank[:, j * NP:(j + 1) * NP], hn[:, i % 8, :], ident[0:NP, 0:NP])
                        last.then_inc(hn_turned.sem, 1)

                def table(q):
                    rhs = {GAT1: gat_w[:, 0, :], GAT2: gat_w[:, 1, :], GCN: wt(W_G),
                           GATV2: wts[:, W_L:W_R + 1, :].rearrange("p n f -> p (n f)"),
                           ATTN: wts[:, W_K:W_Q + 1, :].rearrange("p n f -> p (n f)")}[q]
                    if q == GAT2:
                        pe.wait_ge(fin_out.sem, fin_out.at(GAT1, NCH))
                    else:
                        pe.wait_ge(ht_made.sem, ht_made.at(q, NB))
                    if q == GAT1:
                        pe.wait_ge(prepared, 2)
                    for i in range(NI):
                        if some(i - 3):
                            pe.wait_ge(tab_made.sem, tab_made.at(q, i - 3))
                        bank = b_table[i % 4]
                        mm(bank[0:NP, 0:TF[q]], hT[:, i:NODES:NI], rhs, start=True, stop=True).then_inc(tab_mm.sem, 1)

                def softmax_pass(q):
                    H = HEADS[q]
                    TH = H * GT

                    banks_t = 2 if q in (GAT1, GAT2) else 1

                    def turn_one_hot(gr, t):
                        pe.wait_ge(oh_made.sem, oh_made.at(q, gr.g * 4 + t + 1))
                        if some(gr.g * 4 + t - banks_t + 1):
                            pe.wait_ge(oh_copied.sem, oh_copied.at(q, gr.g * 4 + t - banks_t + 1))
                        pe.sem_inc(waited, 1)
                        for j in range(4):
                            last = tr(p_oht[q][t % 2][0:W, j * P:(j + 1) * P], oh[:, gr.par * GT + 4 * t + j, 0:W], ident_b[:, :])
                        last.then_inc(oh_turned.sem, 1)

                    def edge_features(gr, t):
                        pe.wait_ge(oh_copied.sem, oh_copied.at(q, gr.g * 4 + t + 1))
                        if q == GATV2:
                            pe.wait_ge(ea_in[t].sem, ea_in[t].at(q, gr.g * 16 + 16))
                        if q in (GATV2, ATTN):
                            read = STEPS[q]["add" if q == GATV2 else "times"][t - 2] - (NSTEP[q] if t < 2 else 0)
                            if some(gr.g * NSTEP[q] + read):
                                pe.wait_ge(score_step.sem, score_step.at(q, gr.g * NSTEP[q] + read))
                        if q in (GAT1, GAT2) and t == 0:
                            if some(gr.g):
                                pe.wait_ge(score_sum.sem, score_sum.at(q, gr.g))
                            if some(gr.g * 2):
                                pe.wait_ge(resc_copied.sem, resc_copied.at(q, gr.g * 2))
                        for j in range(4):
                            k = 4 * t + j
                            n = k // path.tiles
                            if k % path.tiles == 0:
                                pe.wait_ge(win_in[n].sem, win_in[n].at(q, gr.g * 16 + 16))
                            e = slice(j * P, (j + 1) * P)
                            slot = gr.par * 4 + n if path is NARROW else n % 8
                            f = p_feat[t % 2][:, e]
                            if q in (GAT1, GAT2):
                                for part in range(3):
                                    last = mm(p_score[:, 4 * k:4 * k + 4], ohT_b[:W, t % 2, e],
                                              win_b[:W, gr.par * GT + n, 4 * part:4 * part + 4],
                                              start=part == 0, stop=part == 2)
                            elif q == GATV2:
                                last = mm(f, turned(path, q, t)[:, e], win[:, slot, :], start=True,
                                          stop=path is NARROW)
                                if path is WIDE:
                                    last = mm(f, ering[0:ED, t % 2, e], we[:, :], start=False, stop=True)
                            else:
                                last = mm(f, turned(path, q, t)[:W, e], win[:W, slot, :], start=True, stop=True)
                        last.then_inc(feat_mm.sem, 1)

                    def aggregate(gr, u):
                        pe.wait_ge(msg_made.sem, msg_made.at(q, gr.g * 4 + u + 1))
                        if u == 0:
                            pe.wait_ge(wm_low.sem, wm_low.at(q, gr.g + 1))
                        pe.wait_ge(oh_widened.sem, oh_widened.at(q, gr.g * 4 + u + 1))
                        if some(sums_free(path, u, gr.g, path.softmax_adds)):
                            pe.wait_ge(added.sem, added.at(q, sums_free(path, u, gr.g, path.softmax_adds)))
                        for j in range(QT):
                            mm(sums_of(path, u, j, ZR)[0], msg[:, u % 2, j, :], oh_wide[:, u % 2, j * P:j * P + W],
                               start=j == 0 or path is WIDE, stop=j == QT - 1 or path is WIDE)
                        for j in range(QT):
                            k = QT * u + j
                            last = mm(sums_of(path, u, j, ZR)[1], wm[:, gr.par, k, :], oh[:, gr.par * GT + k, 0:W],
                                      start=j == 0 or path is WIDE, stop=j == QT - 1 or path is WIDE)
                        last.then_inc(agg_mm.sem, 1)

                    def turn_scores(gr):
                        if q in (GAT1, GAT2):
                            pe.wait_ge(score_out.sem, score_out.at(q, gr.g + 1))
                        else:
                            pe.wait_ge(score_step.sem, score_step.at(q, (gr.g + 1) * NSTEP[q]))
                        pe.sem_inc(waited, 1)
                        tr(p_chunk[0:TH, :], s_sb[:, 0:TH], ident).then_inc(chunk_in.sem, 1)

                    def turn_ends(gr):
                        pe.wait_ge(bwd_made.sem, bwd_made.at(q, gr.g + 1))
                        pe.sem_inc(waited, 1)
                        tr(p_last[:, 0:TH], fwd[0:TH, P - 1:P], ident[0:TH, 0:TH])
                        tr(p_first[:, 0:TH], bwd[0:TH, 0:1], ident[0:TH, 0:TH]).then_inc(last_turned.sem, 1)

                    def turn_carry(gr):
                        pe.wait_ge(carry_out.sem, carry_out.at(q, gr.g * 3 + 3))
                        pe.sem_inc(waited, 1)
                        tr(p_carry[0:TH, :], cshift[:, 0:TH], ident[0:1, 0:1])
                        tr(p_own[0:TH, :], rrow[:, 0:TH], ident[0:1, 0:1])
                        tr(p_next[0:TH, :], rnext[:, 0:TH], ident[0:1, 0:1]).then_inc(carry_turned.sem, 1)

                    def turn_weights(gr):
                        if some(gr.g - 1):
                            pe.wait_ge(wm_rest.sem, wm_rest.at(q, gr.g - 1))
                        if some(gr.g * 4 - 4):
                            pe.wait_ge(msg_made.sem, msg_made.at(q, gr.g * 4 - 4))
                            pe.sem_inc(waited, 1)
                        if q != ATTN:
                            pe.wait_ge(mend_made.sem, mend_made.at(q, gr.g + 1))
                            pe.sem_inc(waited, 1)
                            tr(p_wm[gr.par][:, 64:128], mend[0:TH, :], ident[0:TH, 0:TH])
                        pe.wait_ge(wexp_made.sem, wexp_made.at(q, gr.g + 1))
                        pe.sem_inc(waited, 1)
                        tr(p_wm[gr.par][:, 0:TH], wexp[0:TH, 0:P], ident[0:TH, 0:TH]).then_inc(w_turned.sem, 1)
                        hx = C_HX8 if q == ATTN else C_HX4
                        mm(p_resc, cst[0:TH, hx:hx + P], wexp[0:TH, P:P + 1], start=True, stop=True)
                        mm(p_rescz, cst[0:TH, C_HZ:C_HZ + ZR], wexp[0:TH, P:P + 1], start=True,
                           stop=True).then_inc(resc_mm.sem, 1)

                    def body(gr, before):
                        turn_one_hot(gr, 0)
                        for t in range(4):
                            if t < 3:
                                turn_one_hot(gr, t + 1)
                            edge_features(gr, t)
                            if before is not None and t == (1 if q == ATTN else 2):
                                aggregate(before, 0)
                            if before is not None and t == 3:
                                aggregate(before, 1)
                        turn_scores(gr)
                        turn_ends(gr)
                        if before is not None:
                            aggregate(before, 2)
                        turn_carry(gr)
                        if before is not None:
                            aggregate(before, 3)
                        turn_weights(gr)

                    def tail(gr):
                        for u in range(4):
                            aggregate(gr, u)

                    if q == GATV2 and path is NARROW:
                        pe.wait_ge(we_in, 16)
                    each_group(pe, body, tail)

                def gcn_pass(q):
                    def body(gr, before):
                        pe.wait_ge(ea_in[gr.par].sem, ea_in[gr.par].at(q, gr.half * 16 + 16))
                        for u in range(4):
                            pe.wait_ge(rows_in[gr.par][u].sem, rows_in[gr.par][u].at(q, gr.half * 64 + 64))
                            pe.wait_ge(oh_made.sem, oh_made.at(q, gr.g * 8 + 2 * u + 2))
                            if some(sums_free(path, u, gr.g, path.gcn_adds)):
                                pe.wait_ge(added.sem, added.at(q, sums_free(path, u, gr.g, path.gcn_adds)))
                            for j in range(QT):
                                mm(sums_of(path, u, j, ED)[0], vring[:, gr.par * GT + QT * u + j, 0:D],
                                   oh_gcn[:, u % 2, j * P:j * P + W],
                                   start=j == 0 or path is WIDE, stop=j == QT - 1 or path is WIDE)
                            for j in range(QT):
                                k = QT * u + j
                                last = mm(sums_of(path, u, j, ED)[1], ering[:, gr.par, ED * k:ED * (k + 1)],
                                          ohT[:, u % 2, j * P:j * P + W],
                                          start=j == 0 or path is WIDE, stop=j == QT - 1 or path is WIDE)
                            last.then_inc(agg_mm.sem, 1)

                    each_group(pe, body)

                def banks(c):
                    return psum[0:4] if c % 2 == 0 else psum[4:8]

                def node_products(q):
                    pe.wait_ge(added.sem, added.at(q, path.softmax_adds * GROUPS))
                    for c in range(NCH):
                        hb, sbk, zb, mb = (b[:, 0:CH] for b in banks(c))
                        if some(c - 1):
                            pe.wait_ge(fin_sum.sem, fin_sum.at(q, c - 1))
                        z = zacc[:, chunk(c)]
                        if q == ATTN:
                            mm(zb, cst[0:ZR, C_SZ8:C_SZ8 + P], z, start=True, stop=True).then_inc(fin_mm.sem, 1)
                            continue
                        if q == GATV2:
                            mm(mb[0:ED, :], cst[0:ZR, C_SD:C_SD + ED], z, start=True, stop=True).then_inc(fin_deg.sem, 1)
                            mm(sbk, wt(W_LR), hT[:, chunk(c)], start=True, stop=False)
                            pe.wait_ge(fin_attr.sem, fin_attr.at(q, c + 1))
                            mm(sbk, we[:, :], eacc[:, chunk(c)], start=False, stop=True).then_inc(fin_feat.sem, 1)
                        mm(hb, wt({GAT1: W_1, GAT2: W_2, GATV2: W_L}[q]), hT[:, chunk(c)], start=True, stop=True)
                        mm(zb, cst[0:ZR, C_SZ4:C_SZ4 + P], z, start=True, stop=True)
                        last = mm(mb, cst[0:ZR, C_SM4:C_SM4 + P], z, start=True, stop=True)
                        if q == GATV2:
                            pe.wait_ge(fin_leaky.sem, fin_leaky.at(q, c + 1))
                            last = mm(sbk, att_rep[:, :], kt_sb[:, 0, 0:CH], start=True, stop=True)
                        else:
                            last = mm(sbk, gat_wrep[:, 0 if q == GAT1 else 1, :], hT[:, chunk(c)], start=True,
                                      stop=True)
                        last.then_inc(fin_mm.sem, 1)

                def turn_residual(q):
                    if q == GAT2:
                        pe.wait_ge(fin_out.sem, fin_out.at(q, NCH))
                    elif q == GCN:
                        pe.wait_ge(added.sem, added.at(q, path.gcn_adds * GROUPS))
                    elif q == GATV2:
                        pe.wait_ge(gn_out.sem, gn_out.at(q, 1))
                    else:
                        pe.wait_ge(fin_sum.sem, fin_sum.at(q, NCH))
                    for b in range(NB):
                        if some(b - 1):
                            pe.wait_ge(res_added.sem, res_added.at(q, b - 1))
                        bank = (b_oht, b_feat)[b % 2]
                        for j, i in enumerate(batch(b)):
                            o = bank[0:NP, j * D:(j + 1) * D]
                            if q == ATTN:
                                last = mm(o, acc[:, i:NODES:NI], wt(W_O), start=True, stop=True)
                            else:
                                last = tr(o, acc[:, i:NODES:NI], ident)
                        last.then_inc(res_turned.sem, 1)

                def degrees(q):
                    for i in range(NI):
                        last = tr(b_w[0:NP, 9 * i:9 * i + 9], zacc[0:9, i:NODES:NI], ident[0:9, 0:9])
                    last.then_inc(deg_turned.sem, 1)

                turn_hidden(GAT1)
                table(GAT1)
                softmax_pass(GAT1)
                node_products(GAT1)
                table(GAT2)
                softmax_pass(GAT2)
                node_products(GAT2)
                turn_residual(GAT2)
                degrees(GCN)
                turn_hidden(GCN)
                table(GCN)
                gcn_pass(GCN)
                turn_residual(GCN)
                turn_hidden(GATV2)
                table(GATV2)
                softmax_pass(GATV2)
                node_products(GATV2)
                turn_residual(GATV2)
                turn_hidden(ATTN)
                table(ATTN)
                softmax_pass(ATTN)
                node_products(ATTN)
                turn_residual(ATTN)

            pe.wait_ge(narrow_known, 1)
            all_narrow = pe.value_load(narrow[0:1, 0:1], min_val=0, max_val=1)
            with pe.If(all_narrow > 0):
                layers(NARROW)
            with pe.Else():
                layers(WIDE)

        @block.scalar
        def _(act):
            func = nc.scalar.activation
            act.wait_ge(first_loaded, 16 * FIRST)

            def layers(path):
                W, added = path.nodes, path.added

                def normalize(q):
                    act.wait_ge(ln_var.sem, ln_var.at(q, 1))
                    func(lnv[0:NP, 1, :], lnv[0:NP, 0, :], ACT.Sqrt).then_inc(ln_std.sem, 1)
                    act.wait_ge(ln_stats.sem, ln_stats.at(q, 1))
                    for i in range(NI):
                        if some(i // TB - 1):
                            act.wait_ge(hn_turned.sem, hn_turned.at(q, i // TB - 1))
                        func(hn[:, i % 8, :], x[0:NP, i, :], ACT.Relu, bias=lnv[0:NP, 3, i:i + 1],
                             scale=lnv[0:NP, 2, i:i + 1]).then_inc(hn_made.sem, 1)

                def table(q):
                    for i in range(NI):
                        if q in (GATV2, ATTN):
                            return
                        if i % TC == 0 and (q > 0 or i // TC >= TS):
                            if some(slot_count(q, i // TC)):
                                act.wait_ge(tab_stored[(i // TC) % TS], slot_count(q, i // TC))
                        act.wait_ge(tab_mm.sem, tab_mm.at(q, i + 1))
                        if i == 0 and q == GCN:
                            act.wait_ge(deg_made.sem, deg_made.at(q, 2))
                        bank = b_table[i % 4]
                        o = tab[:, (i // TC) % TS, i % TC, 0:TF[q]]
                        if q == GCN:
                            func(o, bank[0:NP, 0:TF[q]], ACT.Copy, scale=norm[0:NP, 1, i:i + 1]).then_inc(tab_made.sem, 1)
                        else:
                            func(o, bank[0:NP, 0:TF[q]], ACT.Copy).then_inc(tab_made.sem, 1)

                def softmax_pass(q):
                    H = HEADS[q]
                    TH = H * GT

                    def widen(gr, t):
                        if some(gr.g * 4 + t - 1):
                            act.wait_ge(agg_mm.sem, agg_mm.at(q, gr.g * 4 + t - 1))
                        func(oh_wide[:, t % 2, :].rearrange("p (j n) -> p j n", j=QT)[:, :, 0:W],
                             oh[:, gr.par * GT + 4 * t:gr.par * GT + 4 * t + 4, 0:W], ACT.Copy).then_inc(
                            oh_widened.sem, 1)

                    def body(gr, before):
                        for t in range(4):
                            act.wait_ge(oh_turned.sem, oh_turned.at(q, gr.g * 4 + t + 1))
                            if some(gr.g * 4 + turned_before(path, q, t)):
                                act.wait_ge(feat_mm.sem, feat_mm.at(q, gr.g * 4 + turned_before(path, q, t)))
                            func(ohT_b[:W, t % 2, :] if q in (GAT1, GAT2) else turned(path, q, t)[:W, :],
                                 p_oht[q][t % 2][:W, :], ACT.Copy).then_inc(oh_copied.sem, 1)
                            if before is not None and t < 2:
                                widen(before, t)
                        if before is not None:
                            widen(before, 2)
                            widen(before, 3)
                        act.wait_ge(diff_made.sem, diff_made.at(q, gr.g * 2 + 2))
                        if some(gr.g):
                            act.wait_ge(resc_mm.sem, resc_mm.at(q, gr.g))
                        func(wexp[0:TH, :], diff[0:TH, :], ACT.Exp).then_inc(wexp_made.sem, 1)
                        act.wait_ge(w_turned.sem, w_turned.at(q, gr.g + 1))
                        if some(gr.g * 4 - 4):
                            act.wait_ge(agg_mm.sem, agg_mm.at(q, gr.g * 4 - 4))
                        func(wm[:, gr.par, :, 0:8], p_wm[gr.par].rearrange("p (h k) -> p k h", k=GT),
                             ACT.Copy).then_inc(wm_hi.sem, 1)
                        act.wait_ge(resc_mm.sem, resc_mm.at(q, gr.g + 1))
                        A = path.softmax_adds
                        if some(gr.g * A - 2 * A + 2):
                            act.wait_ge(added.sem, added.at(q, gr.g * A - 2 * A + 2))
                        func(resc[:, gr.par, 0:1], p_resc, ACT.Copy).then_inc(resc_copied.sem, 1)
                        func(resc[0:ZR, gr.par, 1:2], p_rescz, ACT.Identity, bias=cst[0:ZR, C_DB:C_DB + 1]).then_inc(resc_copied.sem, 1)
                        act.wait_ge(wm_rest.sem, wm_rest.at(q, gr.g + 1))
                        func(wm[:, gr.par, :, 9:17], wrest[:, :].rearrange("p (h k) -> p k h", k=GT),
                             ACT.Copy).then_inc(wm_mid.sem, 1)

                    def tail(gr):
                        for t in range(4):
                            widen(gr, t)

                    if q == GATV2 and path is NARROW:
                        act.wait_ge(gap_zero, 2)
                    each_group(act, body, tail)

                def node_domain(q):
                    if q == ATTN:
                        return

                    def output(c):
                        act.wait_ge(fin_sum.sem, fin_sum.at(q, c + 1))
                        if q == GAT1:
                            func(hT[:, chunk(c)], temp(c % 2, 6), ACT.Relu, bias=vec[:, V_B1:V_B1 + 1]).then_inc(
                                fin_out.sem, 1)
                        else:
                            b = V_B2 if q == GAT2 else V_BO
                            func(acc[:, chunk(c)], temp(c % 2, 6), ACT.Identity, bias=vec[:, b:b + 1]).then_inc(
                                fin_out.sem, 1)

                    for c in range(NCH + 1):
                        par = c % 2
                        bank = (psum[1] if par == 0 else psum[5])[:, 0:CH]
                        if c < NCH and q == GATV2:
                            act.wait_ge(fin_feat.sem, fin_feat.at(q, c + 1))
                            func(tq_flat[:, 0:CH], bank, ACT.Identity, bias=blr[:, 0:1]).then_inc(fin_biased.sem, 1)
                        if c > 0:
                            output(c - 1)
                        if c < NCH:
                            act.wait_ge(fin_diff.sem, fin_diff.at(q, c + 1))
                            func(temp(par, 2), temp(par, 1), ACT.Relu)
                            func(temp(par, 3), temp(par, 1), ACT.Relu, scale=-1.0).then_inc(fin_parts.sem, 1)
                            act.wait_ge(fin_parts.sem, fin_parts.at(q, c + 1))
                            func(temp(par, 4, 2), temp(par, 2, 2), ACT.Exp, scale=-1.0).then_inc(fin_exp.sem, 1)

                def graph_norm(q):
                    act.wait_ge(gn_mean.sem, gn_mean.at(q, 1))
                    func(vflat[:, 0:NODES], acc[:, 0:NODES], ACT.Square, bias=gn[:, 2:3],
                         accum_out=gn[:, 3:4]).then_inc(gn_sq.sem, 1)
                    act.wait_ge(gn_var.sem, gn_var.at(q, 1))
                    func(gn[:, 5:6], gn[:, 4:5], ACT.Sqrt).then_inc(gn_std.sem, 1)
                    act.wait_ge(gn_scale.sem, gn_scale.at(q, 1))
                    func(acc[:, 0:NODES], acc[:, 0:NODES], ACT.Relu, bias=gn[:, 7:8], scale=gn[:, 6:7]).then_inc(
                        gn_out.sem, 1)

                def degree_root(q):
                    act.wait_ge(deg_made.sem, deg_made.at(q, 1))
                    func(norm[0:NP, 1, :], norm[0:NP, 0, :], ACT.Sqrt).then_inc(deg_root.sem, 1)

                normalize(GAT1)
                table(GAT1)
                softmax_pass(GAT1)
                node_domain(GAT1)
                table(GAT2)
                softmax_pass(GAT2)
                node_domain(GAT2)
                degree_root(GCN)
                normalize(GCN)
                table(GCN)
                normalize(GATV2)
                softmax_pass(GATV2)
                node_domain(GATV2)
                graph_norm(GATV2)
                normalize(ATTN)
                softmax_pass(ATTN)

            act.wait_ge(narrow_known, 1)
            all_narrow = act.value_load(narrow[0:1, 0:1], min_val=0, max_val=1)
            with act.If(all_narrow > 0):
                layers(NARROW)
            with act.Else():
                layers(WIDE)

        @block.vector
        def _(dve):
            v = nc.vector
            chain = [0]

            def step(ins):
                chain[0] += 1
                ins.then_inc(link_sem, 1)
                return chain[0]

            def link(ins):
                chain[0] += 1
                ins.then_inc(link_sem, 1)
                dve.wait_ge(link_sem, chain[0])

            regs = [dve.alloc_register(f"window{k}") for k in range(GT)]

            v.memset(s_tmp[:, :], 0.0).then_inc(setup, 1)
            dve.wait_ge(first_loaded, 16 * FIRST)
            link(v.tensor_tensor(span[:, :], span[:, :], qfirst[:, :], ALU.subtract))
            link(v.tensor_reduce(narrow[:, :], span[:, :], AX_X, ALU.max))
            v.tensor_scalar(narrow[:, :], narrow[:, :], NARROW.nodes, None, ALU.is_lt).then_inc(narrow_known, 1)
            for n, (a, b) in enumerate(((V_AS1, V_AD1), (V_AS2, V_AD2))):
                v.tensor_scalar(gat_cols[:, n, 0:4], cst[:, C_HM4:C_HM4 + 4], vec[:, a:a + 1], None, ALU.mult)
                v.tensor_scalar(gat_cols[:, n, 4:8], cst[:, C_HM4:C_HM4 + 4], vec[:, b:b + 1], None, ALU.mult)
                link(v.tensor_tensor(blr[:, 0:1], vec[:, a:a + 1], vec[:, b:b + 1], ALU.add))
                link(v.tensor_scalar(gat_rep[:, n, :], cst[:, C_SAME:C_SAME + P], blr[:, 0:1], None, ALU.mult))
            v.memset(wm[:, :, :, 0:9], 1.0)
            v.memset(wm[:, :, :, 9:ZR], 0.0)
            v.tensor_copy(iota_b[:, :], cst[:, C_IOTA:C_IOTA + P])
            v.tensor_copy(ident_b[:, :], ident)
            v.memset(rnext[:, :], -BIG)
            v.memset(hT[:, NODES:NCOL], 0.0)
            link(v.tensor_tensor(blr[:, 0:1], vec[:, V_BL:V_BL + 1], vec[:, V_BR:V_BR + 1], ALU.add))
            v.tensor_scalar(att_rep[:, :], cst[:, C_SAME:C_SAME + P], vec[:, V_ATT:V_ATT + 1], None,
                            ALU.mult).then_inc(prepared, 1)
            dve.wait_ge(gat_mm, 2)
            v.tensor_tensor(wts[:, W_LR, :], wts[:, W_L, :], wts[:, W_R, :], ALU.add)
            for n, w in ((0, W_1), (1, W_2)):
                v.tensor_copy(gat_w[:, n, 0:D], wts[:, w, :])
                v.tensor_copy(gat_w[:, n, D:D + 8], b_oht[:, 256 * n:256 * n + 8])
                last = v.tensor_copy(gat_wrep[:, n, :], b_oht[:, 256 * n + 128:256 * n + 256])
            last.then_inc(prepared, 1)

            def penalties():
                a3 = lambda ap: ap.rearrange("p (g e) -> p g e", e=P)
                v.tensor_tensor(a3(start_pen[:, :]), d_cur, d_prev, ALU.not_equal)
                v.tensor_tensor(a3(is_end[:, :]), d_cur, d_next, ALU.not_equal)
                v.tensor_tensor(a3(first_pen[:, :]), d_cur, d_cur[:, :, 0:1].to_broadcast([P, GROUPS, P]),
                                ALU.not_equal)
                v.tensor_tensor(cont_pen[:, :], dfirst[:, :], last_i[:, 1, :], ALU.not_equal)
                v.tensor_tensor(a3(last_pen[:, :]), d_cur, d_cur[:, :, P - 1:P].to_broadcast([P, GROUPS, P]),
                                ALU.not_equal)
                first3 = dfirst[:, :].rearrange("p (g t) -> p g t", t=GT)
                v.memset(row_pen[:, :, :], -BIG)
                link(v.memset(back_pen[:, :, :], 1.0))
                v.tensor_tensor(back_pen[:, :, ::-1][:, :, 0:GT - 1], first3[:, :, 0:GT - 1], first3[:, :, 1:GT],
                                ALU.not_equal)
                link(v.tensor_tensor(last_i[:, 0, :], last_i[:, 0, :], last_i[:, 1, :], ALU.not_equal))
                v.tensor_scalar(end_pen_r, a3(is_end[:, :]), -BIG, None, ALU.mult)
                v.tensor_scalar(start_pen[:, :], start_pen[:, :], -BIG, None, ALU.mult)
                v.tensor_scalar(first_pen[:, :], first_pen[:, :], -BIG, None, ALU.mult)
                v.tensor_scalar(cont_pen[:, :], cont_pen[:, :], -BIG, None, ALU.mult)
                v.tensor_scalar(last_pen[:, :], last_pen[:, :], -BIG, None, ALU.mult)
                v.tensor_scalar(back_pen[:, :, :], back_pen[:, :, :], -BIG, None, ALU.mult)
                v.tensor_scalar(row_pen[:, :, 1:GT + 1], last_i[:, 0, :].rearrange("p (g t) -> p g t", t=GT),
                                -BIG, None, ALU.mult)

            def layers(path):
                W, added = path.nodes, path.added

                def statistics(q):
                    for i in range(NI):
                        last = v.bn_stats(stat[0:NP, i, :], x[0:NP, i, :])
                    link(last)
                    for i in range(NI):
                        last = v.bn_aggr(mv[0:NP, i, :], stat[0:NP, i, :])
                    link(last)
                    v.tensor_scalar(lnv[0:NP, 0, :], mv[0:NP, :, 1], EPS, None, ALU.add).then_inc(ln_var.sem, 1)
                    dve.wait_ge(ln_std.sem, ln_std.at(q, 1))
                    link(v.reciprocal(lnv[0:NP, 2, :], lnv[0:NP, 1, :]))
                    v.scalar_tensor_tensor(out=lnv[0:NP, 3, :], in0=mv[0:NP, :, 0], scalar=-1.0, in1=lnv[0:NP, 2, :],
                                           op0=ALU.mult, op1=ALU.mult).then_inc(ln_stats.sem, 1)

                def hidden(q):
                    cols = hT[:, 0:NODES].rearrange("f (p i) -> f i p", i=NI)
                    for b in range(NB):
                        dve.wait_ge(hn_turned.sem, hn_turned.at(q, b + 1))
                        n = len(batch(b))
                        bank = (b_oht, b_feat)[b % 2]
                        v.tensor_copy(cols[:, TB * b:TB * b + n, :],
                                      bank[:, 0:n * NP].rearrange("f (i p) -> f i p", p=NP)).then_inc(ht_made.sem, 1)

                def table(q):
                    lo, hi = (R_LR, R_KVQ) if q == GATV2 else (R_KVQ, R_O)
                    for i in range(NI):
                        if i % TC == 0:
                            if some(slot_count(q, i // TC)):
                                dve.wait_ge(tab_stored[(i // TC) % TS], slot_count(q, i // TC))
                        dve.wait_ge(tab_mm.sem, tab_mm.at(q, i + 1))
                        bank = b_table[i % 4]
                        v.tensor_tensor(tab[:, (i // TC) % TS, i % TC, 0:TF[q]], bank[0:NP, 0:TF[q]],
                                        brow[0:NP, lo:hi], ALU.add).then_inc(tab_made.sem, 1)

                def split_windows(q):
                    for c in range(TC):
                        s = c % TS
                        dve.wait_ge(tab_made.sem, tab_made.at(q, TC * (c + 1)))
                        if some(slot_count(q, c)):
                            dve.wait_ge(tab_stored[s], slot_count(q, c))
                        a = tab[:, s, :, ROWF[q]:TF[q]]
                        part = [wsplit[:, s, :, 4 * n:4 * n + 4] for n in range(3)]
                        link(v.tensor_copy(part[0], a))
                        link(v.tensor_tensor(wsrest[:, s, :, :], a, part[0], ALU.subtract))
                        link(v.tensor_copy(part[1], wsrest[:, s, :, :]))
                        v.tensor_tensor(part[2], wsrest[:, s, :, :], part[1], ALU.subtract).then_inc(win_split.sem, 1)

                def clear(q):
                    v.memset(acc[:, :], 0.0).then_inc(cleared.sem, 1)
                    if q == GATV2 and path is NARROW:
                        v.memset(ohT[32:ED, :, :], 0.0).then_inc(gap_zero, 1)
                        v.memset(ering[32:ED, :, 0:4 * P], 0.0).then_inc(gap_zero, 1)
                    if q == GCN:
                        v.memset(eacc[:, :], 0.0).then_inc(cleared.sem, 1)
                    else:
                        v.memset(zacc[:, :], 0.0).then_inc(cleared.sem, 1)
                        v.memset(cin[:, :, :], -BIG).then_inc(cleared.sem, 1)
                    dve.wait_ge(cleared.sem, cleared.at(q, 2 if q == GCN else 3))

                def windows(gr):
                    n = GT // path.tiles
                    firsts = qfirst if path is NARROW else dfirst
                    dve.load(regs[0:n], firsts[0:1, bass.ds(gr.g * n, n)])
                    return [dve.snap(r, min_val=0, max_val=NODES) for r in regs[0:n]]

                def one_hots(gr, t, out):
                    d = drel[:, bass.ds(gr.g * GT + QT * t, QT)]
                    return v.tensor_tensor(out, iota_b[:, 0:W].unsqueeze(1).to_broadcast([P, QT, W]),
                                           d.unsqueeze(2).to_broadcast([P, QT, W]), ALU.is_equal)

                def softmax_pass(q):
                    H = HEADS[q]
                    TH = H * GT
                    off = VOFF[q]

                    def hk(ap):
                        return ap.rearrange("p (h k) -> p h k", k=GT)

                    def messages(gr, u):
                        rows = vring[:, gr.par * GT + QT * u:gr.par * GT + QT * (u + 1), off:off + D]
                        w = p_wm[gr.par][:, 0:TH].rearrange("p (h k) -> p k h", k=GT)[:, QT * u:QT * (u + 1), :]
                        if q == ATTN:
                            rows = rows.rearrange("e k (d h) -> e k d h", h=H)
                            w = w.unsqueeze(2).to_broadcast([P, QT, D // H, H])
                            o = msg[:, u % 2, :, :].rearrange("e k (d h) -> e k d h", h=H)
                        else:
                            rows = rows.rearrange("e k (h c) -> e k h c", h=H)
                            w = w.unsqueeze(3).to_broadcast([P, QT, H, D // H])
                            o = msg[:, u % 2, :, :].rearrange("e k (h c) -> e k h c", h=H)
                        if u == 0:
                            dve.wait_ge(wm_mid.sem, wm_mid.at(q, gr.g + 1))
                        dve.wait_ge(rows_in[gr.par][u].sem, rows_in[gr.par][u].at(q, gr.half * 64 + 64))
                        if some(gr.g * 4 + u - 1):
                            dve.wait_ge(agg_mm.sem, agg_mm.at(q, gr.g * 4 + u - 1))
                        v.tensor_tensor(o, rows, w, ALU.mult).then_inc(msg_made.sem, 1)

                    def accumulate(gr, u, starts):
                        A, n = path.softmax_adds, QT // path.tiles
                        if u == 0:
                            dve.wait_ge(resc_copied.sem, resc_copied.at(q, gr.g * 2 + 2))
                            if some(gr.g):
                                dve.wait_ge(added.sem, added.at(q, gr.g * A))
                            a0, z0 = acc[:, bass.ds(starts[0], 1)], zacc[:, bass.ds(starts[0], 1)]
                            v.tensor_tensor(a0, a0, resc[:, gr.par, 0:1], ALU.mult).then_inc(added.sem, 1)
                            v.tensor_tensor(z0, z0, resc[0:ZR, gr.par, 1:2], ALU.mult).then_inc(added.sem, 1)
                        dve.wait_ge(agg_mm.sem, agg_mm.at(q, gr.g * 4 + u + 1))
                        for j in range(n):
                            i = gr.g * A + 2 + 2 * (n * u + j)
                            sa, sz = sums_of(path, u, j, ZR)
                            aw, zw = acc[:, bass.ds(starts[n * u + j], W)], zacc[:, bass.ds(starts[n * u + j], W)]
                            dve.wait_ge(added.sem, added.at(q, i - 1))
                            v.tensor_tensor(aw, aw, sa, ALU.add).then_inc(added.sem, 1)
                            dve.wait_ge(added.sem, added.at(q, i))
                            v.tensor_tensor(zw, zw, sz, ALU.add).then_inc(added.sem, 1)

                    def edge_scores(gr, t, step):
                        base, at = gr.g * NSTEP[q], STEPS[q]
                        f, act_f = tq_sb[:, t % 2, :], kt_sb[:, t % 2, :]
                        tiles = lambda ap: ap.rearrange("e (k f) -> e k f", f=D)
                        keys = vring[:, gr.par * GT + QT * t:gr.par * GT + QT * (t + 1), 0:D]
                        if step == ("add" if q == GATV2 else "times"):
                            dve.wait_ge(feat_mm.sem, feat_mm.at(q, gr.g * 4 + t + 1))
                            dve.wait_ge(rows_in[gr.par][t].sem, rows_in[gr.par][t].at(q, gr.half * 64 + 64))
                            if t > 1:
                                dve.wait_ge(score_step.sem, score_step.at(q, base + at["sum"][t - 2]))
                        if step == "add":
                            last = v.tensor_tensor(tiles(f), tiles(p_feat[t % 2][:, :]), keys, ALU.add)
                        elif step == "leaky":
                            dve.wait_ge(score_step.sem, score_step.at(q, base + at["add"][t]))
                            last = v.scalar_tensor_tensor(out=act_f, in0=f, scalar=NEG, in1=f, op0=ALU.mult,
                                                          op1=ALU.max)
                        elif step == "times" and q == GATV2:
                            dve.wait_ge(score_step.sem, score_step.at(q, base + at["leaky"][t]))
                            last = v.tensor_tensor(tiles(f), tiles(act_f), brow[:, R_ATT:R_ATT + D].unsqueeze(
                                1).to_broadcast([P, QT, D]), ALU.mult)
                        elif step == "times":
                            last = v.scalar_tensor_tensor(out=tiles(f), in0=tiles(p_feat[t % 2][:, :]), scalar=0.25,
                                                          in1=keys, op0=ALU.mult, op1=ALU.mult)
                        else:
                            dve.wait_ge(score_step.sem, score_step.at(q, base + at["times"][t]))
                            if t == 0:
                                if some(gr.g):
                                    dve.wait_ge(chunk_in.sem, chunk_in.at(q, gr.g))
                            parts = (tiles(f).rearrange("e k (h c) -> e k h c", h=H) if q == GATV2 else
                                     tiles(f).rearrange("e k (d h) -> e k h d", h=H))
                            last = v.tensor_reduce(
                                s_sb[:, 0:TH].rearrange("p (h k) -> p k h", k=GT)[:, QT * t:QT * (t + 1), :],
                                parts, AX_X, ALU.add)
                        last.then_inc(score_step.sem, 1)

                    def scores(gr):
                        if q in (GAT1, GAT2):
                            dve.wait_ge(feat_mm.sem, feat_mm.at(q, gr.g * 4 + 4))
                            dve.wait_ge(rows_in[gr.par][3].sem, rows_in[gr.par][3].at(q, gr.half * 64 + 64))
                            for b in range(3):
                                dve.wait_ge(rows_in[gr.par][b].sem, rows_in[gr.par][b].at(q, gr.half * 64 + 64))
                            v.tensor_tensor(hk(s_tmp[:, 0:TH]), p_score[:, 0:TH].rearrange("p (k h) -> p h k", h=H),
                                            vring[:, gr.par * GT:(gr.par + 1) * GT, D:D + 4].rearrange("p k h -> p h k"),
                                            ALU.add).then_inc(score_sum.sem, 1)
                            dve.wait_ge(score_sum.sem, score_sum.at(q, gr.g + 1))
                            if some(gr.g):
                                dve.wait_ge(chunk_in.sem, chunk_in.at(q, gr.g))
                            v.scalar_tensor_tensor(out=s_sb[:, 0:TH], in0=s_tmp[:, 0:TH], scalar=NEG,
                                                   in1=s_tmp[:, 0:TH], op0=ALU.mult, op1=ALU.max).then_inc(
                                score_out.sem, 1)

                    def carry(gr):
                        pen = bass.ds(gr.g * P, P)
                        dve.wait_ge(chunk_in.sem, chunk_in.at(q, gr.g + 1))
                        if some(gr.g):
                            dve.wait_ge(last_turned.sem, last_turned.at(q, gr.g))
                        v.tensor_tensor_scan(fwd[0:TH, :], start_pen[0:TH, pen], p_chunk[0:TH, :], -BIG,
                                             ALU.add, ALU.max).then_inc(fwd_made.sem, 1)
                        dve.wait_ge(fwd_made.sem, fwd_made.at(q, gr.g + 1))
                        v.tensor_tensor_scan(bwd[0:TH, ::-1], end_pen[0:TH, pen], fwd[0:TH, ::-1], -BIG,
                                             ALU.add, ALU.max).then_inc(bwd_made.sem, 1)
                    def row_pens(gr):
                        if some(gr.g):
                            dve.wait_ge(own_made.sem, own_made.at(q, gr.g))
                        v.tensor_copy(row_pen_h[:, 0:H * (GT + 1)].rearrange("p (h k) -> p h k", h=H),
                                      row_pen[:, bass.ds(gr.g, 1), :].to_broadcast([1, H, GT + 1])).then_inc(
                            pens_made.sem, 1)
                        v.tensor_copy(hk(back_pen_h[:, 0:TH]),
                                      back_pen[:, bass.ds(gr.g, 1), :].to_broadcast([1, H, GT])).then_inc(
                            pens_made.sem, 1)

                    def rows(gr):
                        tiles = bass.ds(gr.g * GT, GT)
                        one_row = lambda ap: ap.rearrange("p h k -> p (h k)")
                        dve.wait_ge(last_turned.sem, last_turned.at(q, gr.g + 1))
                        if some(gr.g * 3):
                            dve.wait_ge(carry_out.sem, carry_out.at(q, gr.g * 3))
                        v.tensor_copy(cin[:, 0:H, 1:GT + 1], hk(p_last[:, 0:TH])).then_inc(last_copied.sem, 1)
                        dve.wait_ge(last_copied.sem, last_copied.at(q, gr.g + 1))
                        dve.wait_ge(pens_made.sem, pens_made.at(q, gr.g * 2 + 2))
                        v.tensor_tensor_scan(one_row(crow[:, 0:H, :]), row_pen_h[:, 0:H * (GT + 1)],
                                             one_row(cin[:, 0:H, :]), -BIG, ALU.add, ALU.max).then_inc(carry_made.sem, 1)
                        dve.wait_ge(carry_made.sem, carry_made.at(q, gr.g + 1))
                        if some(gr.g):
                            dve.wait_ge(carry_turned.sem, carry_turned.at(q, gr.g))
                        v.tensor_tensor(hk(cshift[:, 0:TH]), crow[:, 0:H, 0:GT],
                                        cont_pen[:, tiles].unsqueeze(1).to_broadcast([1, H, GT]),
                                        ALU.add).then_inc(carry_out.sem, 1)
                        v.tensor_copy(cin[:, 0:H, 0:1], crow[:, 0:H, GT:GT + 1]).then_inc(carry_out.sem, 1)
                        dve.wait_ge(carry_out.sem, carry_out.at(q, gr.g * 3 + 1))
                        v.tensor_tensor(first_row[:, 0:TH], p_first[:, 0:TH], cshift[:, 0:TH], ALU.max).then_inc(
                            row_made.sem, 1)
                        dve.wait_ge(row_made.sem, row_made.at(q, gr.g + 1))
                        v.tensor_tensor_scan(rrow[:, 0:TH][:, ::-1], back_pen_h[:, 0:TH], first_row[:, 0:TH][:, ::-1],
                                             -BIG, ALU.add, ALU.max).then_inc(own_made.sem, 1)
                        dve.wait_ge(own_made.sem, own_made.at(q, gr.g + 1))
                        v.tensor_tensor(hk(rnext[:, 0:TH])[:, :, 0:GT - 1], hk(rrow[:, 0:TH])[:, :, 1:GT],
                                        cont_pen[:, bass.ds(gr.g * GT + 1, GT - 1)].unsqueeze(1).to_broadcast(
                                            [1, H, GT - 1]), ALU.add).then_inc(carry_out.sem, 1)

                    def weigh(gr):
                        pen = bass.ds(gr.g * P, P)
                        dve.wait_ge(carry_turned.sem, carry_turned.at(q, gr.g + 1))
                        v.scalar_tensor_tensor(out=shift[0:TH, :], in0=first_pen[0:TH, pen], scalar=p_own[0:TH, :],
                                               in1=bwd[0:TH, :], op0=ALU.add, op1=ALU.max).then_inc(shift_part.sem, 1)
                        dve.wait_ge(shift_part.sem, shift_part.at(q, gr.g + 1))
                        v.scalar_tensor_tensor(out=shift[0:TH, :], in0=last_pen[0:TH, pen], scalar=p_next[0:TH, :],
                                               in1=shift[0:TH, :], op0=ALU.add, op1=ALU.max).then_inc(shift_made.sem, 1)
                        dve.wait_ge(shift_made.sem, shift_made.at(q, gr.g + 1))
                        if some(gr.g):
                            dve.wait_ge(wexp_made.sem, wexp_made.at(q, gr.g))
                        v.tensor_tensor(diff[0:TH, 0:P], p_chunk[0:TH, :], shift[0:TH, :], ALU.subtract).then_inc(
                            diff_made.sem, 1)
                        v.tensor_tensor(diff[0:TH, P:P + 1], p_carry[0:TH, :], shift[0:TH, 0:1],
                                        ALU.subtract).then_inc(diff_made.sem, 1)
                        if q != ATTN:
                            if some(gr.g):
                                dve.wait_ge(w_turned.sem, w_turned.at(q, gr.g))
                            v.tensor_tensor(mend[0:TH, :], shift[0:TH, :], is_end[0:TH, pen], ALU.mult).then_inc(
                                mend_made.sem, 1)

                    def split_rest(gr):
                        dve.wait_ge(wm_hi.sem, wm_hi.at(q, gr.g + 1))
                        if some(gr.g):
                            dve.wait_ge(wm_low.sem, wm_low.at(q, gr.g))
                        hi = wm[:, gr.par, :, 0:8].rearrange("p k h -> p h k")
                        v.tensor_tensor(wrest[:, :].rearrange("p (h k) -> p h k", k=GT),
                                        p_wm[gr.par].rearrange("p (h k) -> p h k", k=GT), hi,
                                        ALU.subtract).then_inc(wm_rest.sem, 1)

                    def split_low(gr):
                        dve.wait_ge(wm_mid.sem, wm_mid.at(q, gr.g + 1))
                        mid = wm[:, gr.par, :, 9:17]
                        v.tensor_tensor(wm[:, gr.par, :, 18:26], wrest[:, :].rearrange("p (h k) -> p k h", k=GT),
                                        mid, ALU.subtract).then_inc(wm_low.sem, 1)

                    def body(gr, before):
                        for t in range(4):
                            one_hots(gr, t, oh[:, gr.par * GT + QT * t:gr.par * GT + QT * (t + 1), 0:W]).then_inc(
                                oh_made.sem, 1)
                        if before is not None:
                            messages(before, 0)
                            messages(before, 1)
                        row_pens(gr)
                        starts = windows(before) if before is not None else None
                        if q in (GAT1, GAT2):
                            scores(gr)
                        elif q == GATV2:
                            for t in range(5):
                                if t < 4:
                                    edge_scores(gr, t, "add")
                                if t > 0:
                                    edge_scores(gr, t - 1, "times")
                                if t < 4:
                                    edge_scores(gr, t, "leaky")
                                if t > 0:
                                    edge_scores(gr, t - 1, "sum")
                        else:
                            for t in range(5):
                                if t < 4:
                                    edge_scores(gr, t, "times")
                                if t > 0:
                                    edge_scores(gr, t - 1, "sum")
                        if before is not None:
                            accumulate(before, 0, starts)
                        carry(gr)
                        if before is not None:
                            messages(before, 2)
                            accumulate(before, 1, starts)
                        rows(gr)
                        if before is not None:
                            messages(before, 3)
                            accumulate(before, 2, starts)
                        weigh(gr)
                        if before is not None:
                            accumulate(before, 3, starts)
                        split_rest(gr)
                        split_low(gr)

                    def tail(gr):
                        starts = windows(gr)
                        for u in range(4):
                            messages(gr, u)
                            if u > 0:
                                accumulate(gr, u - 1, starts)
                        accumulate(gr, 3, starts)

                    each_group(dve, body, tail)
                    dve.wait_ge(added.sem, added.at(q, path.softmax_adds * GROUPS))

                def gcn_pass(q):
                    def body(gr, before):
                        starts = windows(gr)
                        n = QT // path.tiles

                        def accumulate(u):
                            dve.wait_ge(agg_mm.sem, agg_mm.at(q, gr.g * 4 + u + 1))
                            for j in range(n):
                                i = gr.g * path.gcn_adds + 2 * (n * u + j)
                                sa, se = sums_of(path, u, j, ED)
                                aw, ewn = acc[:, bass.ds(starts[n * u + j], W)], eacc[:, bass.ds(starts[n * u + j], W)]
                                if some(i - 1):
                                    dve.wait_ge(added.sem, added.at(q, i - 1))
                                v.tensor_tensor(aw, aw, sa, ALU.add).then_inc(added.sem, 1)
                                if some(i):
                                    dve.wait_ge(added.sem, added.at(q, i))
                                v.tensor_tensor(ewn, ewn, se, ALU.add).then_inc(added.sem, 1)

                        for u in range(4):
                            if some(gr.g * 4 + u - 1):
                                dve.wait_ge(agg_mm.sem, agg_mm.at(q, gr.g * 4 + u - 1))
                            bare = ohT[:, u % 2, :].rearrange("p (j n) -> p j n", j=QT)[:, :, 0:W]
                            weighed = oh_gcn[:, u % 2, :].rearrange("p (j n) -> p j n", j=QT)[:, :, 0:W]
                            one_hots(gr, u, bare).then_inc(oh_made.sem, 1)
                            dve.wait_ge(oh_made.sem, oh_made.at(q, gr.g * 8 + 2 * u + 1))
                            v.tensor_tensor(weighed, bare,
                                            ew[:, bass.ds(gr.g * GT + QT * u, QT)].unsqueeze(2).to_broadcast([P, QT, W]),
                                            ALU.mult).then_inc(oh_made.sem, 1)
                            if u > 0:
                                accumulate(u - 1)
                        accumulate(3)

                    each_group(dve, body)
                    dve.wait_ge(added.sem, added.at(q, path.gcn_adds * GROUPS))

                def node_domain(q):
                    def attributes(c):
                        mb = (psum[3] if c % 2 == 0 else psum[7])[0:ED, 0:CH]
                        dve.wait_ge(fin_deg.sem, fin_deg.at(q, c + 1))
                        link(v.tensor_scalar(temp(c % 2, 1)[0:ED, :], mb, 1.0, None, ALU.max))
                        link(v.reciprocal(temp(c % 2, 1)[0:ED, :], temp(c % 2, 1)[0:ED, :]))
                        v.tensor_tensor(eacc[:, chunk(c)], eacc[:, chunk(c)], temp(c % 2, 1)[0:ED, :],
                                        ALU.mult).then_inc(fin_attr.sem, 1)

                    def leaky(c):
                        dve.wait_ge(fin_biased.sem, fin_biased.at(q, c + 1))
                        f = tq_flat[:, 0:CH]
                        v.scalar_tensor_tensor(out=kt_sb[:, 0, 0:CH], in0=f, scalar=NEG, in1=f, op0=ALU.mult,
                                               op1=ALU.max).then_inc(fin_leaky.sem, 1)

                    def difference(c):
                        par = c % 2
                        _, sbk, _, mb = (b[:, 0:CH] for b in (psum[0:4] if par == 0 else psum[4:8]))
                        dve.wait_ge(fin_mm.sem, fin_mm.at(q, c + 1))
                        if q == GATV2:
                            link(v.tensor_copy(temp(par, 0), sbk))
                        else:
                            link(v.tensor_scalar(temp(par, 0), sbk, 0.0, NEG, ALU.min, ALU.mult))
                            link(v.scalar_tensor_tensor(out=temp(par, 0), in0=sbk, scalar=0.0, in1=temp(par, 0),
                                                        op0=ALU.max, op1=ALU.add))
                        v.tensor_tensor(temp(par, 1), temp(par, 0), mb, ALU.subtract).then_inc(fin_diff.sem, 1)

                    def combine(c):
                        par = c % 2
                        hb, _, zb, _ = (b[:, 0:CH] for b in (psum[0:4] if par == 0 else psum[4:8]))
                        ea, eb, z = temp(par, 4), temp(par, 5), temp(par, 1)
                        dve.wait_ge(fin_exp.sem, fin_exp.at(q, c + 1))
                        z_scaled = step(v.tensor_tensor(z, zb, ea, ALU.mult))
                        edges = step(v.tensor_tensor(temp(par, 7), acc[:, chunk(c)], ea, ALU.mult))
                        dve.wait_ge(link_sem, z_scaled)
                        z_made = step(v.scalar_tensor_tensor(out=z, in0=z, scalar=1e-16, in1=eb, op0=ALU.add,
                                                             op1=ALU.add))
                        if q == GATV2:
                            loop = step(v.scalar_tensor_tensor(out=temp(par, 0), in0=hb, scalar=vec[:, V_BL:V_BL + 1],
                                                               in1=eb, op0=ALU.add, op1=ALU.mult))
                        else:
                            loop = step(v.tensor_tensor(temp(par, 0), hb, eb, ALU.mult))
                        dve.wait_ge(link_sem, z_made)
                        inverse = step(v.reciprocal(z, z))
                        dve.wait_ge(link_sem, max(edges, loop))
                        total = step(v.tensor_tensor(temp(par, 7), temp(par, 7), temp(par, 0), ALU.add))
                        dve.wait_ge(link_sem, max(inverse, total))
                        if some(c - 1):
                            dve.wait_ge(fin_out.sem, fin_out.at(q, c - 1))
                        v.tensor_tensor(temp(par, 6), temp(par, 7), z, ALU.mult).then_inc(fin_sum.sem, 1)

                    for c in range(NCH + 1):
                        if c < NCH:
                            if q == GATV2:
                                attributes(c)
                        if c > 0:
                            combine(c - 1)
                        if c < NCH:
                            if q == GATV2:
                                leaky(c)
                            difference(c)
                    dve.wait_ge(fin_out.sem, fin_out.at(q, NCH))

                def divide(q):
                    for c in range(NCH):
                        zb = (psum[2] if c % 2 == 0 else psum[6])[:, 0:CH]
                        r = temp(c % 2, 0)
                        dve.wait_ge(fin_mm.sem, fin_mm.at(q, c + 1))
                        link(v.tensor_scalar(r, zb, 1e-30, None, ALU.max))
                        link(v.reciprocal(r, r))
                        v.tensor_tensor(acc[:, chunk(c)], acc[:, chunk(c)], r, ALU.mult).then_inc(fin_sum.sem, 1)

                def graph_norm(q):
                    link(v.tensor_reduce(gn[:, 0:1], acc[:, 0:NODES], AX_X, ALU.add))
                    link(v.tensor_scalar(gn[:, 1:2], gn[:, 0:1], -1.0 / NODES, None, ALU.mult))
                    v.tensor_tensor(gn[:, 2:3], gn[:, 1:2], vec[:, V_GM:V_GM + 1], ALU.mult).then_inc(gn_mean.sem, 1)
                    dve.wait_ge(gn_sq.sem, gn_sq.at(q, 1))
                    v.tensor_scalar(gn[:, 4:5], gn[:, 3:4], 1.0 / NODES, EPS, ALU.mult, ALU.add).then_inc(gn_var.sem, 1)
                    dve.wait_ge(gn_std.sem, gn_std.at(q, 1))
                    link(v.reciprocal(gn[:, 5:6], gn[:, 5:6]))
                    link(v.tensor_tensor(gn[:, 6:7], gn[:, 5:6], vec[:, V_GW:V_GW + 1], ALU.mult))
                    v.scalar_tensor_tensor(out=gn[:, 7:8], in0=gn[:, 6:7], scalar=gn[:, 2:3],
                                           in1=vec[:, V_GB:V_GB + 1], op0=ALU.mult, op1=ALU.add).then_inc(
                        gn_scale.sem, 1)

                def residual(q):
                    for b in range(NB):
                        n = len(batch(b))
                        i0 = TB * b
                        bank = (b_oht, b_feat)[b % 2]
                        got = bank[0:NP, 0:n * D].rearrange("p (i f) -> p i f", f=D)
                        xs = x[0:NP, i0:i0 + n, :]
                        dve.wait_ge(res_turned.sem, res_turned.at(q, b + 1))
                        if q == GCN:
                            for j in range(n):
                                link(v.scalar_tensor_tensor(out=temp(0, j)[0:NP, 0:D], in0=got[:, j, :],
                                                            scalar=norm[0:NP, 1, i0 + j:i0 + j + 1],
                                                            in1=brow[0:NP, R_G:R_G + D], op0=ALU.mult, op1=ALU.add))
                                last = v.scalar_tensor_tensor(out=x[0:NP, i0 + j, :], in0=temp(0, j)[0:NP, 0:D],
                                                              scalar=0.0, in1=x[0:NP, i0 + j, :], op0=ALU.max,
                                                              op1=ALU.add)
                        elif q == ATTN:
                            if some(b - 1):
                                dve.wait_ge(res_added.sem, res_added.at(q, b - 1))
                            t = temp(b % 2, 0, 2)[0:NP, 0:n * D].rearrange("p (i f) -> p i f", f=D)
                            link(v.tensor_tensor(t, got, brow[0:NP, R_O:R_O + D].unsqueeze(1).to_broadcast([NP, n, D]),
                                                 ALU.add))
                            last = v.tensor_tensor(xs, xs, t, ALU.add)
                        else:
                            last = v.tensor_tensor(xs, xs, got, ALU.add)
                        last.then_inc(res_added.sem, 1)
                    dve.wait_ge(res_added.sem, res_added.at(q, NB))

                def degrees(q):
                    dve.wait_ge(deg_turned.sem, deg_turned.at(q, 1))
                    v.tensor_scalar(norm[0:NP, 0, :], b_w[0:NP, 0:9 * NI].rearrange("p (i z) -> p i z", z=9)[:, :, 8],
                                    1.0, None, ALU.max).then_inc(deg_made.sem, 1)
                    dve.wait_ge(deg_root.sem, deg_root.at(q, 1))
                    v.reciprocal(norm[0:NP, 1, :], norm[0:NP, 1, :]).then_inc(deg_made.sem, 1)
                    dve.wait_ge(deg_made.sem, deg_made.at(q, 2))

                statistics(GAT1)
                hidden(GAT1)
                dve.wait_ge(loaded, 16 * LOADS)
                split_windows(GAT1)
                penalties()
                firsts = dfirst_b[:, :]
                if path is NARROW:
                    firsts = firsts.rearrange("p (u t) -> p u t", t=QT)[:, :, 0:1].to_broadcast(
                        [P, TILES // QT, QT])
                    v.tensor_tensor(drel[:, :].rearrange("p (u t) -> p u t", t=QT),
                                    dtile[:, :].rearrange("p (u t) -> p u t", t=QT), firsts,
                                    ALU.subtract).then_inc(drel_made, 1)
                else:
                    v.tensor_tensor(drel[:, :], dtile[:, :], firsts, ALU.subtract).then_inc(drel_made, 1)
                dve.wait_ge(drel_made, 1)
                clear(GAT1)
                softmax_pass(GAT1)
                node_domain(GAT1)
                split_windows(GAT2)
                clear(GAT2)
                softmax_pass(GAT2)
                node_domain(GAT2)
                residual(GAT2)
                degrees(GCN)
                statistics(GCN)
                hidden(GCN)
                clear(GCN)
                gcn_pass(GCN)
                residual(GCN)
                statistics(GATV2)
                hidden(GATV2)
                table(GATV2)
                clear(GATV2)
                softmax_pass(GATV2)
                node_domain(GATV2)
                graph_norm(GATV2)
                residual(GATV2)
                statistics(ATTN)
                hidden(ATTN)
                table(ATTN)
                clear(ATTN)
                softmax_pass(ATTN)
                divide(ATTN)
                residual(ATTN)

            dve.wait_ge(narrow_known, 1)
            all_narrow = dve.value_load(narrow[0:1, 0:1], min_val=0, max_val=1)
            before_layers = chain[0]
            with dve.If(all_narrow > 0):
                layers(NARROW)
            chain[0] = before_layers
            with dve.Else():
                layers(WIDE)



def kernel(**inputs):
    import numpy as np
    import concourse.bacc as bacc
    from concourse.bass_utils import run_bass_kernel_spmd as run

    arr = {k: np.ascontiguousarray(a) for k, a in inputs.items()}
    pad = EPAD - EDGES
    dst = np.concatenate([arr["dst"], np.full(pad, NODES, np.int32)])
    src = np.concatenate([arr["src"], np.zeros(pad, np.int32)])
    attr = np.concatenate([arr["edge_attr_64"], np.zeros((pad, ED), np.float32)])
    ew = np.concatenate([arr["edge_weight1"][:, 0], np.zeros(pad, np.float32)])
    edge_of = np.array([-1], np.int32)
    f = np.arange(P)
    cst = np.zeros((P, C_END), np.float32)
    cst[:, C_ID:C_ID + P] = np.eye(P)
    cst[:, C_IOTA:C_IOTA + P] = f[None, :]
    cst[:, C_SAME:C_SAME + P] = f[:, None] // 32 == f[None, :] // 32
    cst[:, C_HM4:C_HM4 + 4] = f[:, None] // 32 == f[None, 0:4]
    cst[:, C_HM8:C_HM8 + 8] = f[:, None] % 8 == f[None, 0:8]
    cst[:, C_HX4:C_HX4 + P] = (f[:, None] // GT == f[None, :] // 32) & (f[:, None] % GT == 0)
    cst[:, C_HX8:C_HX8 + P] = (f[:, None] // GT == f[None, :] % 8) & (f[:, None] % GT == 0)
    cst[:, C_HZ:C_HZ + ZR] = (f[:, None] // GT == f[None, 0:ZR] % 9) & (f[:, None] % GT == 0)
    z = f[0:ZR, None] % 9
    cst[0:ZR, C_SZ4:C_SZ4 + P] = z == f[None, :] // 32
    cst[0:ZR, C_SM4:C_SM4 + P] = z - 4 == f[None, :] // 32
    cst[0:ZR, C_SD:C_SD + P] = z == 8
    cst[0:ZR, C_SZ8:C_SZ8 + P] = z == f[None, :] % 8
    cst[0:ZR, C_DB:C_DB + 1] = z == 8
    w = np.concatenate([
        arr["L0_gnn_W1"], arr["L0_gnn_W1"].T, arr["L0_gnn_W2"], arr["L0_gnn_W2"].T, arr["L1_gnn_W"],
        arr["L2_gnn_Wl"], arr["L2_gnn_Wr"], arr["L3_gnn_Wk"].T, arr["L3_gnn_Wv"].T, arr["L3_gnn_Wq"].T,
        arr["L3_gnn_Wo"].T], axis=1)
    vec = np.stack([arr[n].reshape(-1) for n in (
        "L0_gnn_a_src1", "L0_gnn_a_dst1", "L0_gnn_b1", "L0_gnn_a_src2", "L0_gnn_a_dst2", "L0_gnn_b2",
        "L2_gnn_bl", "L2_gnn_br", "L2_gnn_att", "L2_gnn_bias_out", "L2_gnn_gn_weight", "L2_gnn_gn_bias",
        "L2_gnn_gn_mean_scale")], axis=1)
    rows = np.concatenate([arr[n] for n in (
        "L1_gnn_b", "L2_gnn_bl", "L2_gnn_br", "L3_gnn_bk", "L3_gnn_bv", "L3_gnn_bq", "L3_gnn_bo")]
                          + [arr["L2_gnn_att"].reshape(-1)])[None, :]
    data = {
        "x": arr["x"],
        "src_idx": src.reshape(TILES, P).T,
        "dst_tile": dst.reshape(TILES, P).T,
        "dst_first": dst[::P][None, :],
        "quarter_first": dst[::QT * P][None, :],
        "quarter_last": dst[QT * P - 1::QT * P][None, :],
        "dst_last": dst[P - 1::P][None, :],
        "dst_last_prev": np.concatenate([edge_of, dst[P - 1:-1:P]])[None, :],
        "dst_flat": np.concatenate([edge_of, dst, edge_of]),
        "edge_attr": attr.reshape(TILES, P, ED).transpose(1, 0, 2).reshape(P, TILES * ED),
        "edge_attr_t": attr.T,
        "edge_weight": ew.reshape(TILES, P).T,
        "weights": w, "w_edge": arr["L2_gnn_We"], "vectors": vec, "bias_rows": rows, "consts": cst,
    }
    nc = bacc.Bacc("TRN2", target_bir_lowering=False, num_devices=1)
    arrays, args = {}, []
    for name, a in data.items():
        a = np.ascontiguousarray(a)
        arrays[f"in_{name}_dram"] = a
        args.append(nc.dram_tensor(f"in_{name}_dram", a.shape, mybir.dt.from_np(a.dtype), kind="ExternalInput").ap())
    args.append(nc.dram_tensor("out_0_dram", (NODES, D), F32, kind="ExternalOutput").ap())
    build(nc, *args)
    r = run(nc, [arrays], core_ids=[0])
    return r.results[0]["out_0_dram"]
```
